# Optimizing a Trainium2 kernel written in Bass

```python
import numpy as np
import jax
import jax.numpy as jnp

def _softmax(x, axis=-1):
    return jax.nn.softmax(x, axis=axis)

def _gelu(x):
    return jax.nn.gelu(x, approximate=True)

def _silu(x):
    return jax.nn.silu(x)

def _sigmoid(x):
    return jax.nn.sigmoid(x)

def _layernorm(x, axis=-1, eps=1e-05):
    m = jnp.mean(x, axis=axis, keepdims=True)
    v = jnp.var(x, axis=axis, keepdims=True)
    return (x - m) / jnp.sqrt(v + eps)

def _scatter_add(tgt, idx, src, axis=0):
    return tgt.at[idx].add(src)

def _segment_sum(src, seg, n):
    return jax.ops.segment_sum(src, seg, n)
kernel_name = 'mk_macaron_d1_jaxref_r8_8e3625'

def setup_inputs(seed: int=0):
    np.random.seed(seed)
    _w = jnp.asarray

    def _L0_attn_setup():
        import jax, jax.numpy as jnp
        import numpy as np
        B, S, D = (4, 512, 128)
        H = 8
        DK = D // H
        DV = D // H
        KLEPE = 5
        ROPE_BASE = 10000.0

        def rotate_half(x):
            x1, x2 = jnp.split(x, 2, axis=-1)
            return jnp.concatenate([-x2, x1], axis=-1)

        def rope_sin_cos(seq_len, dim):
            inv_freq = 1.0 / ROPE_BASE ** (jnp.arange(0, dim, 2, dtype=jnp.float32) / dim)
            freqs = jnp.arange(seq_len, dtype=jnp.float32)[:, None] * inv_freq[None, :]
            emb = jnp.concatenate([freqs, freqs], axis=-1)
            return (jnp.sin(emb), jnp.cos(emb))

        def mala_attn(q, k, v):
            sin, cos = rope_sin_cos(q.shape[1], q.shape[-1])
            sin, cos = (sin[None, :, None, :], cos[None, :, None, :])
            q = q * cos + rotate_half(q) * sin
            k = k * cos + rotate_half(k) * sin
            scale = q.shape[-1] ** (-0.5)
            seq_len = q.shape[1]
            kv = jnp.einsum('bshd,bshe->bhde', k, v)
            ksum = k.sum(axis=1)
            vsum = v.sum(axis=1)
            num = jnp.einsum('bshd,bhde->bshe', q, kv) * scale + vsum[:, None, :, :]
            den = jnp.einsum('bshd,bhd->bsh', q, ksum) * scale + seq_len
            return num / den[..., None]

        def lepe_conv(v, w, b):
            Bb, Ss = (v.shape[0], v.shape[1])
            x = v.transpose(0, 2, 3, 1).reshape(Bb, H * DV, Ss)
            y = jax.lax.conv_general_dilated(x, w, window_strides=(1,), padding=[(KLEPE // 2, KLEPE // 2)], dimension_numbers=('NCH', 'OIH', 'NCH'), feature_group_count=H * DV)
            y = y + b[None, :, None]
            return y.reshape(Bb, H, DV, Ss).transpose(0, 3, 1, 2)
        key = jax.random.key(seed)
        ks = jax.random.split(key, 8)
        w = 0.02
        return {'hidden_states': jax.random.normal(ks[0], (B, S, D), dtype=jnp.float32), 'Wq': jax.random.normal(ks[1], (D, D), dtype=jnp.float32) * w, 'Wk': jax.random.normal(ks[2], (D, D), dtype=jnp.float32) * w, 'Wv': jax.random.normal(ks[3], (D, D), dtype=jnp.float32) * w, 'Wg': jax.random.normal(ks[4], (D, D), dtype=jnp.float32) * w, 'Wo': jax.random.normal(ks[5], (D, D), dtype=jnp.float32) * w, 'lepe_w': jax.random.normal(ks[6], (D, 1, KLEPE), dtype=jnp.float32) * 0.1, 'lepe_b': jnp.zeros((D,), dtype=jnp.float32)}
    _L0_attn_in = _L0_attn_setup()

    def _L0_ffn_setup():
        import jax, jax.numpy as jnp
        import numpy as np
        D_MODEL = 128
        HIDDEN = 512
        N_EXPERTS = 8
        key = jax.random.key(seed)
        ks = jax.random.split(key, 7)
        B, S = (4, 256)
        s_in = 1.0 / np.sqrt(D_MODEL)
        s_hid = 1.0 / np.sqrt(HIDDEN)
        return {'x': jax.random.normal(ks[0], (B, S, D_MODEL), dtype=jnp.float32), 'Wr': jax.random.uniform(ks[1], (D_MODEL, N_EXPERTS), jnp.float32, -s_in, s_in), 'br': jax.random.uniform(ks[2], (N_EXPERTS,), jnp.float32, -s_in, s_in), 'W1': jax.random.uniform(ks[3], (N_EXPERTS, D_MODEL, HIDDEN), jnp.float32, -s_in, s_in), 'b1': jax.random.uniform(ks[4], (N_EXPERTS, HIDDEN), jnp.float32, -s_in, s_in), 'W2': jax.random.uniform(ks[5], (N_EXPERTS, HIDDEN, D_MODEL), jnp.float32, -s_hid, s_hid), 'b2': jax.random.uniform(ks[6], (N_EXPERTS, D_MODEL), jnp.float32, -s_hid, s_hid)}
    _L0_ffn_in = _L0_ffn_setup()
    _d = {'L0_attn_hidden_states': _L0_attn_in['hidden_states'], 'L0_attn_Wq': _L0_attn_in['Wq'], 'L0_attn_Wk': _L0_attn_in['Wk'], 'L0_attn_Wv': _L0_attn_in['Wv'], 'L0_attn_Wg': _L0_attn_in['Wg'], 'L0_attn_Wo': _L0_attn_in['Wo'], 'L0_attn_lepe_w': _L0_attn_in['lepe_w'], 'L0_attn_lepe_b': _L0_attn_in['lepe_b'], 'L0_ffn_Wr': _L0_ffn_in['Wr'], 'L0_ffn_br': _L0_ffn_in['br'], 'L0_ffn_W1': _L0_ffn_in['W1'], 'L0_ffn_b1': _L0_ffn_in['b1'], 'L0_ffn_W2': _L0_ffn_in['W2'], 'L0_ffn_b2': _L0_ffn_in['b2']}
    _x0 = _d['L0_attn_hidden_states']
    _d['L0_attn_hidden_states'] = jax.random.normal(jax.random.fold_in(jax.random.key(seed), 1), (8, 256, 128), dtype=_x0.dtype)
    del _x0
    return _d

def reference(L0_attn_hidden_states, L0_attn_Wq, L0_attn_Wk, L0_attn_Wv, L0_attn_Wg, L0_attn_Wo, L0_attn_lepe_w, L0_attn_lepe_b, L0_ffn_Wr, L0_ffn_br, L0_ffn_W1, L0_ffn_b1, L0_ffn_W2, L0_ffn_b2):

    def _L0_attn_ref(hidden_states, Wq, Wk, Wv, Wg, Wo, lepe_w, lepe_b):
        import jax, jax.numpy as jnp
        import numpy as np
        B, S, D = (4, 512, 128)
        H = 8
        DK = D // H
        DV = D // H
        KLEPE = 5
        ROPE_BASE = 10000.0

        def rotate_half(x):
            x1, x2 = jnp.split(x, 2, axis=-1)
            return jnp.concatenate([-x2, x1], axis=-1)

        def rope_sin_cos(seq_len, dim):
            inv_freq = 1.0 / ROPE_BASE ** (jnp.arange(0, dim, 2, dtype=jnp.float32) / dim)
            freqs = jnp.arange(seq_len, dtype=jnp.float32)[:, None] * inv_freq[None, :]
            emb = jnp.concatenate([freqs, freqs], axis=-1)
            return (jnp.sin(emb), jnp.cos(emb))

        def mala_attn(q, k, v):
            sin, cos = rope_sin_cos(q.shape[1], q.shape[-1])
            sin, cos = (sin[None, :, None, :], cos[None, :, None, :])
            q = q * cos + rotate_half(q) * sin
            k = k * cos + rotate_half(k) * sin
            scale = q.shape[-1] ** (-0.5)
            seq_len = q.shape[1]
            kv = jnp.einsum('bshd,bshe->bhde', k, v)
            ksum = k.sum(axis=1)
            vsum = v.sum(axis=1)
            num = jnp.einsum('bshd,bhde->bshe', q, kv) * scale + vsum[:, None, :, :]
            den = jnp.einsum('bshd,bhd->bsh', q, ksum) * scale + seq_len
            return num / den[..., None]

        def lepe_conv(v, w, b):
            Bb, Ss = (v.shape[0], v.shape[1])
            x = v.transpose(0, 2, 3, 1).reshape(Bb, H * DV, Ss)
            y = jax.lax.conv_general_dilated(x, w, window_strides=(1,), padding=[(KLEPE // 2, KLEPE // 2)], dimension_numbers=('NCH', 'OIH', 'NCH'), feature_group_count=H * DV)
            y = y + b[None, :, None]
            return y.reshape(Bb, H, DV, Ss).transpose(0, 3, 1, 2)
        Bb, Ss, _ = hidden_states.shape
        q = (hidden_states @ Wq.T).reshape(Bb, Ss, H, DK)
        k = (hidden_states @ Wk.T).reshape(Bb, Ss, H, DK)
        v = (hidden_states @ Wv.T).reshape(Bb, Ss, H, DV)
        o_gate = hidden_states @ Wg.T
        o = mala_attn(q, k, v) + lepe_conv(v, lepe_w, lepe_b)
        o = o.reshape(Bb, Ss, H * DV) * o_gate
        return o @ Wo.T

    def _L0_ffn_ref(x, Wr, br, W1, b1, W2, b2):
        import jax, jax.numpy as jnp
        import numpy as np
        D_MODEL = 128
        HIDDEN = 512
        N_EXPERTS = 8
        router_logits = x @ Wr + br
        router_probs = jax.nn.softmax(router_logits, axis=-1)
        top_probs = jnp.max(router_probs, axis=-1, keepdims=True)
        top_idx = jnp.argmax(router_probs, axis=-1)
        h = jax.nn.gelu(jnp.einsum('bsd,edh->bseh', x, W1) + b1, approximate=False)
        expert_out = jnp.einsum('bseh,ehd->bsed', h, W2) + b2
        chosen = jnp.take_along_axis(expert_out, top_idx[..., None, None], axis=2)
        chosen = jnp.squeeze(chosen, axis=2)
        return chosen * top_probs
    x = L0_attn_hidden_states
    x = x + 0.5 * _L0_ffn_ref(_layernorm(x, axis=-1), L0_ffn_Wr, L0_ffn_br, L0_ffn_W1, L0_ffn_b1, L0_ffn_W2, L0_ffn_b2)
    x = x + _L0_attn_ref(_layernorm(x, axis=-1), L0_attn_Wq, L0_attn_Wk, L0_attn_Wv, L0_attn_Wg, L0_attn_Wo, L0_attn_lepe_w, L0_attn_lepe_b)
    x = x + 0.5 * _L0_ffn_ref(_layernorm(x, axis=-1), L0_ffn_Wr, L0_ffn_br, L0_ffn_W1, L0_ffn_b1, L0_ffn_W2, L0_ffn_b2)
    return x

_drawn_inputs = setup_inputs


def setup_inputs(seed=0):
    import zlib

    import numpy as np

    out = dict(_drawn_inputs(seed))
    spreads = {'L0_attn_lepe_b': (0.0, 0.8)}
    factors = {'L0_attn_Wq': 8.0,
     'L0_attn_Wk': 8.0,
     'L0_attn_Wv': 8.0,
     'L0_attn_Wg': 8.0,
     'L0_attn_Wo': 8.0,
     'L0_attn_lepe_w': 8.0,
     'L0_ffn_br': 4.713,
     'L0_ffn_b1': 8.0,
     'L0_ffn_b2': 7.962}
    for name, (base, spread) in spreads.items():
        noise = np.random.default_rng([zlib.crc32(name.encode()), seed]).standard_normal(out[name].shape)
        drawn = base * np.exp(spread * noise) if base else spread * noise
        out[name] = jnp.asarray(drawn.astype(out[name].dtype))
    for name, factor in factors.items():
        out[name] = (out[name] * factor).astype(out[name].dtype)
    return out
```

```python
from contextlib import ExitStack

import numpy as np

import concourse.bass as bass
from concourse import mybir

P = 128
D = 128
TOKENS, SEQ = 2048, 256
HEADS, DK = 8, 16
EXPERTS, HIDDEN = 8, 512
HC = HIDDEN // P
GROUPS = 2
GT = TOKENS // GROUPS // P
GE = GT * EXPERTS
GTILES = (TOKENS // GROUPS - EXPERTS) // P + EXPERTS
NT = GROUPS * GTILES
SLOTS = NT * P
RING = 3
HALF = 512
TAPS = 5
EPS = 1e-5
WSCALE = 64.0
AW = HC * P * 2 + P
BW = HC * P * 2 + P

F32, F16, BF16 = mybir.dt.float32, mybir.dt.float16, mybir.dt.bfloat16
I32, U32 = mybir.dt.int32, mybir.dt.uint32
ALU = mybir.AluOpType
ACT = mybir.ActivationFunctionType
X = mybir.AxisListType.X

C_ID, C_MASK, C_COST, C_SINT = 0, 128, 256, 512
C_COSR, C_SINR, C_RANK, C_TILE, C_PART, C_END = 768, 1024, 1280, 1288, 1288 + GTILES, 1290 + GTILES


def constants():
    f = np.zeros((P, C_END), np.float32)
    f[:, C_ID:C_ID + P] = np.eye(P)
    head = np.arange(P) // DK
    f[:, C_MASK:C_MASK + P] = (head[:, None] == head[None, :]) * np.float32(DK ** -0.5)
    inv = (1.0 / np.float32(10000.0) ** (np.arange(0, DK, 2, dtype=np.float32) / np.float32(DK))).astype(np.float32)
    ang = np.arange(SEQ, dtype=np.float32)[:, None] * inv[None, :]
    ang = np.tile(np.concatenate([ang, ang], axis=1), (1, HEADS))
    sign = np.where(np.arange(P) % DK < DK // 2, -1.0, 1.0).astype(np.float32)
    cos, sin = np.cos(ang).astype(np.float32), np.sin(ang).astype(np.float32) * sign[None, :]
    f[:, C_COST:C_COST + SEQ], f[:, C_SINT:C_SINT + SEQ] = cos.T, sin.T
    f[:, C_COSR:C_COSR + SEQ] = cos.reshape(2, P, P).transpose(1, 0, 2).reshape(P, SEQ)
    f[:, C_SINR:C_SINR + SEQ] = sin.reshape(2, P, P).transpose(1, 0, 2).reshape(P, SEQ)
    f[:, C_RANK:C_RANK + EXPERTS] = EXPERTS - np.arange(EXPERTS)
    f[:, C_TILE:C_TILE + GTILES] = np.arange(GTILES)
    part = np.zeros(P, np.int64)
    part[4:8], part[97], part[8:12], part[98] = 1, 1, 2, 2
    f[:, C_PART] = -(part >= 1).astype(np.float32)
    f[:, C_PART + 1] = -(part >= 2).astype(np.float32)
    h = np.zeros((P, 3 * P + HIDDEN), np.float16)
    h[:, 0:P] = np.eye(P)
    h[:, P:2 * P] = np.triu(np.ones((P, P)), 1)
    h[:, 2 * P:3 * P] = 1
    for r in range(3 * HC):
        h[r, 3 * P + (r % HC) * P:3 * P + (r % HC + 1) * P] = 1
    return f, h


def program(nc, x_in, wr_in, br_in, w1_in, b1_in, w2_in, b2_in, wattn_in, lepe_in, cf_in, ch_in, out):
    with ExitStack() as ctx:
        def sb(name, shape, dt=F32):
            return ctx.enter_context(nc.sbuf_tensor(name, shape, dt))

        def sem(name):
            return ctx.enter_context(nc.semaphore(name))

        sorted_x = [nc.dram_tensor(f"sorted_x{g}", [GTILES * P, 2 * D], F16, kind="Internal").ap() for g in range(GROUPS)]
        sorted_y = [nc.dram_tensor(f"sorted_y{g}", [GTILES * P, D], F32, kind="Internal").ap() for g in range(GROUPS)]

        bank = [ctx.enter_context(nc.psum_tensor(f"bank{i}", [P, 512], F32)) for i in range(8)]

        cf, ch = sb("cf", [P, C_END]), sb("ch", [P, 3 * P + HIDDEN], F16)
        ident, mask = cf[:, C_ID:C_ID + P], cf[:, C_MASK:C_MASK + P]
        rank = cf[:, C_RANK:C_RANK + EXPERTS]
        ident16, before, ones16, chunk_sel = ch[:, 0:P], ch[:, P:2 * P], ch[:, 2 * P:3 * P], ch[:, 3 * P:]
        x = sb("x", [P, GROUPS * GT, D])
        wr, br = sb("wr", [P, EXPERTS]), sb("br", [P, EXPERTS])
        wattn = sb("wattn", [P, 7, P])
        lepe = sb("lepe", [P, TAPS + 1])
        w1f, w2f = sb("w1f", [P, EXPERTS, HIDDEN]), sb("w2f", [P, EXPERTS, HIDDEN])
        bf, bres = sb("bf", [P, EXPERTS, P]), sb("bres", [P, EXPERTS, P])
        bhi = sb("bhi", [P, EXPERTS, P], BF16)
        tabA, tabB = sb("tabA", [P, EXPERTS, AW], F16), sb("tabB", [P, EXPERTS, BW], F16)
        zeros = sb("zeros", [P, 2 * D], F16)

        bn, mv = sb("bn", [P, GT, 6]), sb("mv", [P, GT, 2])
        std, rstd, eps = sb("std", [P, GT]), sb("rstd", [P, GT]), sb("eps", [P, 1])
        xn = sb("xn", [P, GT, D])
        xs = [sb(f"xs{g}", [P, GT, 2 * D], F16) for g in range(GROUPS)]
        xnT = [sb(f"xnT{g}", [P, GT * P]) for g in range(GROUPS)]
        lg, top, ld = sb("lg", [P, GT, EXPERTS]), sb("top", [P, GT]), sb("ld", [P, GT, EXPERTS])
        score, best = sb("score", [P, GT, EXPERTS]), sb("best", [P, GT])
        onehot = sb("onehot", [P, GT, EXPERTS], F16)
        ex, exsum = sb("ex", [P, GT, EXPERTS]), sb("exsum", [P, GT])
        coef = [sb(f"coef{g}", [P, GT]) for g in range(GROUPS)]
        cnt, tiles = sb("cnt", [P, EXPERTS], I32), sb("tiles", [P, EXPERTS], I32)
        cum, first = sb("cum", [P, EXPERTS]), sb("first", [P, EXPERTS])
        posw, posf = sb("posw", [P, GT, EXPERTS]), sb("posf", [P, GT])
        pos = [sb(f"pos{g}", [P, GT], U32) for g in range(GROUPS)]
        over, owner = sb("over", [1, GTILES, EXPERTS]), sb("owner", [1, GTILES])
        expert = [sb(f"expert{g}", [1, GTILES], I32) for g in range(GROUPS)]
        ones1 = sb("ones1", [P, EXPERTS])

        ringA, ringB = sb("ringA", [P, RING, AW], F16), sb("ringB", [P, RING, BW], F16)
        ringX, ringT = sb("ringX", [P, RING, 2 * D], F16), sb("ringT", [P, RING, 2 * P], F16)
        act = sb("act", [P, RING, HIDDEN])
        acth, actl = sb("acth", [P, RING, HIDDEN], F16), sb("actl", [P, RING, HIDDEN], F16)
        ybuf = sb("ybuf", [P, RING, D])
        yback = [sb(f"yback{g}", [P, GT, D]) for g in range(GROUPS)]

        t1, t2, t3, t4 = (sb(f"t{i}", [P, HALF]) for i in range(4))
        qr, kr = sb("qr", [P, HALF]), sb("kr", [P, HALF])
        vpad, vsum = sb("vpad", [P, 2, SEQ + TAPS - 1]), sb("vsum", [P, 2])
        gate = sb("gate", [P, HALF])
        vrow = sb("vrow", [P, 4, P + 1])
        kvm, ksm = sb("kvm", [P, 2, P]), sb("ksm", [P, 2, P])
        den, rden = sb("den", [P, 2, SEQ]), sb("rden", [P, 2, SEQ])
        local, att = sb("local", [P, 2, SEQ]), sb("att", [P, 2, SEQ])
        gated = sb("gated", [P, HALF])
        seqlen = sb("seqlen", [P, 1])

        x_in_sem = [sem(f"x_loaded{g}") for g in range(GROUPS)]
        consts_loaded, attn_loaded, w1_loaded, w2_loaded = (
            sem(n) for n in ("consts_loaded", "attn_loaded", "w1_loaded", "w2_loaded"))
        bias_zeroed, bias_loaded = sem("bias_zeroed"), sem("bias_loaded")
        zeros_set, slots_cleared, pool_set = sem("zeros_set"), sem("slots_cleared"), sem("pool_set")
        hi_ready, tables_ready = sem("hi_ready"), sem("tables_ready")
        stats_ready, std_ready, xn_ready = sem("stats_ready"), sem("std_ready"), sem("xn_ready")
        xn_turned, xnT_ready = sem("xn_turned"), sem("xnT_ready")
        logits_ready, shifted_ready, exp_ready = sem("logits_ready"), sem("shifted_ready"), sem("exp_ready")
        onehot_ready, ranks_ready = sem("onehot_ready"), sem("ranks_ready")
        pos_ready, expert_ready, xs_ready = sem("pos_ready"), sem("expert_ready"), sem("xs_ready")
        sorted_done = [sem(f"sorted_done{g}") for g in range(GROUPS)]
        back_done = [[sem(f"back_done{g}_{t}") for t in range(GT)] for g in range(GROUPS)]
        a_landed = [sem(f"a_landed{s}") for s in range(RING)]
        b_landed = [sem(f"b_landed{s}") for s in range(RING)]
        x_landed = [sem(f"x_landed{s}") for s in range(RING)]
        y_stored = [sem(f"y_stored{s}") for s in range(RING)]
        tile_turned, tileT_ready = sem("tile_turned"), sem("tileT_ready")
        hid_ready, gelu_ready = sem("hid_ready"), sem("gelu_ready")
        acth_ready, actl_ready = sem("acth_ready"), sem("actl_ready")
        y_ready, y_copied = sem("y_ready"), sem("y_copied")
        q_ready, v_ready, gate_ready, k_ready, vrow_ready = (
            sem(n) for n in ("q_ready", "v_ready", "gate_ready", "k_ready", "vrow_ready"))
        qr_ready, kr_ready, vpad_ready, gate_copied, vrow_copied = (
            sem(n) for n in ("qr_ready", "kr_ready", "vpad_ready", "gate_copied", "vrow_copied"))
        kv_ready, kvm_ready, nd_ready, den_copied, att_ready = (
            sem(n) for n in ("kv_ready", "kvm_ready", "nd_ready", "den_copied", "att_ready"))
        gated_ready, proj_ready, x_updated = sem("gated_ready"), sem("proj_ready"), sem("x_updated")
        x_final, stored = sem("x_final"), sem("stored")
        dve_step, pool_step = sem("dve_step"), sem("pool_step")

        NORM = {(0, 0): 0, (0, 1): 1, ("a", 0): 2, (1, 0): 3, ("a", 1): 4, (1, 1): 5}

        def ahead(i, s, d):
            return i + (s + d) // RING, (s + d) % RING

        block = ctx.enter_context(nc.Block())

        @block.sync
        def _(sp):
            for g in range(GROUPS):
                sp.dma_start(x[:, g * GT:(g + 1) * GT, :],
                             x_in[g * GT * P:(g + 1) * GT * P, :].rearrange("(t p) d -> p t d", p=P)
                             ).then_inc(x_in_sem[g], 16)
                if g == 0:
                    sp.dma_start(cf[:], cf_in).then_inc(consts_loaded, 16)
                    sp.dma_start(ch[:], ch_in).then_inc(consts_loaded, 16)
                    sp.dma_start(wr[:], wr_in).then_inc(consts_loaded, 16)
                    sp.dma_start(br[:], br_in.to_broadcast([P, EXPERTS])).then_inc(consts_loaded, 16)
            sp.dma_start(w1f[:], w1_in.rearrange("e d h -> d e h")).then_inc(w1_loaded, 16)
            sp.dma_start(w2f[:].rearrange("p e (c d) -> p e c d", c=HC),
                         w2_in.rearrange("e (c p) d -> p e c d", p=P)).then_inc(w2_loaded, 16)
            sp.wait_ge(bias_zeroed, 1)
            for k in range(3):
                sp.dma_start(bf[HC * k:HC * (k + 1)],
                             b1_in.rearrange("e (c p) -> c e p", p=P)).then_inc(bias_loaded, 16)
                sp.dma_start(bf[96 + k:97 + k], b2_in.rearrange("(a e) d -> a e d", a=1)).then_inc(bias_loaded, 16)
            sp.dma_start(wattn[:], wattn_in).then_inc(attn_loaded, 16)
            sp.dma_start(lepe[:], lepe_in).then_inc(attn_loaded, 16)
            sp.wait_ge(zeros_set, 1)
            for g in range(GROUPS):
                sp.dma_start(sorted_x[g].rearrange("(n p) d -> p n d", p=P),
                             zeros[:, None, :].to_broadcast([P, GTILES, 2 * D])).then_inc(slots_cleared, 16)

            def expert_of(i, s, g):
                off = i * RING + (s - g * GTILES)
                where = bass.ds(off, 1) if not isinstance(off, int) else slice(off, off + 1)
                return sp.value_load(expert[g][0:1, where], min_val=0, max_val=EXPERTS - 1)

            def load_a(f, i, s, g, free):
                e = expert_of(i, s, g)
                if free:
                    sp.wait_ge(hid_ready, f * NT + i * RING + (s - RING + 1))
                sp.dma_start(ringA[:, s, :], tabA[:, bass.ds(e, 1), :]).then_inc(a_landed[s], 16)

            def load_b(f, i, s, g, free):
                e = expert_of(i, s, g)
                if free:
                    sp.wait_ge(y_ready, f * NT + i * RING + (s - RING + 1))
                sp.dma_start(ringB[:, s, :], tabB[:, bass.ds(e, 1), :]).then_inc(b_landed[s], 16)

            def load_x(f, i, s, g, free):
                if free:
                    sp.wait_ge(tile_turned, f * NT + i * RING + (s - RING + 1))
                row = i * (RING * P) + (s - g * GTILES) * P
                sp.dma_start(ringX[:, s, :], sorted_x[g][bass.ds(row, P), :]).then_inc(x_landed[s], 16)

            def store_y(f, i, s, g):
                sp.wait_ge(y_copied, f * NT + i * RING + (s + 1))
                row = i * (RING * P) + (s - g * GTILES) * P
                sp.dma_start(sorted_y[g][bass.ds(row, P), :], ybuf[:, s, :]).then_inc(y_stored[s], 16)

            def step(f, i, s, m, last=NT):
                if m is None or m + 3 < NT:
                    ia, sa = ahead(i, s, 3)
                    ga = g_of(m, 3)
                    load_a(f, ia, sa, ga, True)
                    load_x(f, ia, sa, ga, True)
                if m is None or m + 1 < NT:
                    ib, s_b = ahead(i, s, 1)
                    load_b(f, ib, s_b, g_of(m, 1), f > 0 or m is None or m + 1 >= RING)
                if m is None or m >= 2:
                    store_y(f, *ahead(i, s, -2), g_of(m, -2))

            def g_of(m, d):
                return cur[0] if m is None else (m + d) // GTILES

            cur = [0]
            sp.wait_ge(tables_ready, 5)
            for f in range(2):
                sp.wait_ge(expert_ready, GROUPS * f + 1)
                sp.wait_ge(sorted_done[0], 16 * GT * (f + 1))
                for s in range(RING):
                    load_a(f, 0, s, 0, f > 0)
                    load_x(f, 0, s, 0, f > 0)
                load_b(f, 0, 0, 0, f > 0)
                for m in range(3):
                    step(f, m // RING, m % RING, m)
                cur[0] = 0
                with sp.Fori(1, 4) as i:
                    for s in range(RING):
                        step(f, i, s, None)
                sp.wait_ge(expert_ready, GROUPS * f + 2)
                sp.wait_ge(sorted_done[1], 16 * GT * (f + 1))
                for m in range(12, 18):
                    step(f, m // RING, m % RING, m)
                cur[0] = 1
                with sp.Fori(6, 9) as i:
                    for s in range(RING):
                        step(f, i, s, None)
                for m in range(27, NT + 2):
                    step(f, m // RING, m % RING, m)
            for g in range(GROUPS):
                for t in range(0, GT, 2):
                    n = g * GT + t
                    sp.wait_ge(x_final, n + 2)
                    sp.dma_start(out[n * P:(n + 2) * P, :].rearrange("(t p) d -> p t d", p=P),
                                 x[:, n:n + 2, :]).then_inc(stored, 16)
            sp.wait_ge(stored, 16 * GROUPS * GT // 2)

        @block.gpsimd
        def _(pool):
            nc.gpsimd.memset(bf[:], 0.0).then_inc(bias_zeroed, 1)
            nc.gpsimd.memset(zeros[:], 0.0).then_inc(zeros_set, 1)
            nc.gpsimd.memset(vpad[:], 0.0)
            nc.gpsimd.memset(ones1[:], 1.0)
            nc.gpsimd.memset(eps[:], EPS)
            nc.gpsimd.memset(seqlen[:], float(SEQ))
            nc.gpsimd.memset(vrow[:], 1.0).then_inc(pool_set, 1)

            def sort_out(f, g):
                pool.wait_ge(pos_ready, GROUPS * f + g + 1)
                pool.wait_ge(xs_ready, GROUPS * f + g + 1)
                for t in range(GT):
                    nc.gpsimd.indirect_dma_start(
                        out=sorted_x[g], out_offset=bass.IndirectOffsetOnAxis(ap=pos[g][:, t:t + 1], axis=0),
                        in_=xs[g][:, t, :], in_offset=None).then_inc(sorted_done[g], 16)

            def sort_back(f, g):
                for s in range(RING):
                    pool.wait_ge(y_stored[s], 16 * (f * NT + (g + 1) * GTILES) // RING)
                for t in range(GT):
                    nc.gpsimd.indirect_dma_start(
                        out=yback[g][:, t, :], out_offset=None, in_=sorted_y[g],
                        in_offset=bass.IndirectOffsetOnAxis(ap=pos[g][:, t:t + 1], axis=0)).then_inc(back_done[g][t], 16)

            pool.wait_ge(slots_cleared, 16 * GROUPS)
            for f in range(2):
                for g in range(GROUPS):
                    sort_out(f, g)
                for g in range(GROUPS):
                    sort_back(f, g)

        @block.scalar
        def _(sc):
            def norm(k, g):
                sc.wait_ge(stats_ready, k + 1)
                nc.scalar.activation(std[:], mv[:, :, 1], ACT.Sqrt, bias=eps[:]).then_inc(std_ready, 1)
                for h in range(2):
                    sc.wait_ge(xn_turned, 2 * k + h + 1)
                    nc.scalar.copy(xnT[g][:, h * HALF:(h + 1) * HALF], bank[6 + h][:]).then_inc(xnT_ready, 1)

            def route(f, g):
                sc.wait_ge(shifted_ready, GROUPS * f + g + 1)
                nc.scalar.activation(ex[:], ld[:], ACT.Exp).then_inc(exp_ready, 1)

            def turn_copy(f, i, s):
                n = f * NT + i * RING + s
                sc.wait_ge(tile_turned, n + 1)
                if not isinstance(i, int) or i > 0 or f > 0:
                    sc.wait_ge(hid_ready, n + (1 - RING))
                nc.scalar.copy(ringT[:, s, :], bank[6 + s % 2][:, 0:P].bitcast(F16)).then_inc(tileT_ready, 1)

            def gelu(f, i, s):
                n = f * NT + i * RING + s
                sc.wait_ge(hid_ready, n + 1)
                if not isinstance(i, int) or i > 0 or f > 0:
                    sc.wait_ge(actl_ready, n + (1 - RING))
                nc.scalar.activation(act[:, s, :], bank[s][:], ACT.Gelu, scale=1.0 / WSCALE).then_inc(gelu_ready, 1)

            def experts(f):
                for s in range(RING):
                    turn_copy(f, 0, s)
                for s in range(2):
                    gelu(f, 0, s)
                for s in range(RING):
                    turn_copy(f, 1, s)
                    gelu(f, *ahead(0, s, 2))
                with sc.Fori(1, NT // RING - 1) as i:
                    for s in range(RING):
                        turn_copy(f, i + 1, s)
                        gelu(f, *ahead(i, s, 2))
                gelu(f, NT // RING - 1, 2)

            def attend(g, h):
                a = 2 * g + h
                sc.wait_ge(v_ready, a + 1)
                for b in range(2):
                    last = nc.scalar.activation(vpad[:, b, 2:2 + SEQ], bank[2][:, b * SEQ:(b + 1) * SEQ], ACT.Copy,
                                                accum_out=vsum[:, b:b + 1])
                last.then_inc(vpad_ready, 1)
                sc.wait_ge(gate_ready, a + 1)
                nc.scalar.copy(gate[:], bank[3][:]).then_inc(gate_copied, 1)
                sc.wait_ge(vrow_ready, a + 1)
                nc.scalar.copy(vrow[:, :, 0:P], bank[6][:].rearrange("p (t c) -> p t c", t=4)).then_inc(vrow_copied, 1)
                for b in range(2):
                    sc.wait_ge(nd_ready, 2 * a + b + 1)
                    nc.scalar.activation(den[:, b, :], bank[4 + b][:, SEQ:2 * SEQ], ACT.Identity,
                                         bias=seqlen[:]).then_inc(den_copied, 1)

            sc.wait_ge(w1_loaded, 16)
            sc.wait_ge(pool_set, 1)
            norm(0, 0)
            route(0, 0)
            for tab, raw, loaded in ((tabA, w1f, w1_loaded), (tabB, w2f, w2_loaded)):
                sc.wait_ge(loaded, 16)
                nc.scalar.activation(tab[:, :, 0:HIDDEN], raw[:], ACT.Copy, scale=WSCALE).then_inc(hi_ready, 1)
            norm(1, 1)
            route(0, 1)
            experts(0)
            for g in range(GROUPS):
                norm(NORM["a", g], g)
                for h in range(2):
                    attend(g, h)
                norm(NORM[1, g], g)
                route(1, g)
            experts(1)

        @block.vector
        def _(v):
            steps = [0]

            def link(ins):
                steps[0] += 1
                ins.then_inc(dve_step, 1)
                v.wait_ge(dve_step, steps[0])

            def norm(k, g):
                for t in range(GT):
                    last = nc.vector.bn_stats(bn[:, t, :], x[:, g * GT + t, :])
                link(last)
                for t in range(GT):
                    last = nc.vector.bn_aggr(mv[:, t, :], bn[:, t, :])
                last.then_inc(stats_ready, 1)
                v.wait_ge(std_ready, k + 1)
                if k:
                    v.wait_ge(xn_turned, 2 * k)
                link(nc.vector.reciprocal(rstd[:], std[:]))
                for t in range(GT):
                    last = nc.vector.tensor_scalar(xn[:, t, :], x[:, g * GT + t, :], mv[:, t, 0:1], rstd[:, t:t + 1],
                                                   ALU.subtract, ALU.mult)
                    if t % 4 == 3:
                        last.then_inc(xn_ready, 1)

            def split(k, f, g):
                v.wait_ge(xn_ready, 2 * k + 2)
                link(nc.vector.tensor_copy(xs[g][:, :, 0:D], xn[:]))
                nc.vector.tensor_tensor(xs[g][:, :, D:2 * D], xn[:], xs[g][:, :, 0:D], ALU.subtract).then_inc(xs_ready, 1)

            def route(f, g):
                n = GROUPS * f + g
                v.wait_ge(logits_ready, n + 1)
                all3 = [P, GT, EXPERTS]
                link(nc.vector.tensor_tensor(lg[:], bank[5][:, 0:GE].rearrange("p (t e) -> p t e", t=GT),
                                             br[:, None, :].to_broadcast(all3), ALU.add))
                link(nc.vector.tensor_reduce(top[:], lg[:], X, ALU.max))
                nc.vector.tensor_tensor(ld[:], lg[:], top[:, :, None].to_broadcast(all3), ALU.subtract).then_inc(shifted_ready, 1)
                v.wait_ge(shifted_ready, n + 1)
                link(nc.vector.scalar_tensor_tensor(out=score[:], in0=ld[:], scalar=0.0, in1=rank[:, None, :].to_broadcast(all3),
                                                    op0=ALU.is_ge, op1=ALU.mult))
                link(nc.vector.tensor_reduce(best[:], score[:], X, ALU.max))
                nc.vector.tensor_tensor(onehot[:], score[:], best[:, :, None].to_broadcast(all3), ALU.is_equal).then_inc(onehot_ready, 1)
                v.wait_ge(exp_ready, n + 1)
                link(nc.vector.tensor_reduce(exsum[:], ex[:], X, ALU.add))
                link(nc.vector.reciprocal(best[:], exsum[:]))
                link(nc.vector.tensor_scalar(coef[g][:], best[:], 0.5, None, ALU.mult))
                v.wait_ge(ranks_ready, n + 1)
                link(nc.vector.tensor_scalar(cnt[:], bank[4][:, GE:GE + EXPERTS], float(P - 1), None, ALU.add))
                link(nc.vector.tensor_scalar(tiles[:], cnt[:], P.bit_length() - 1, None, ALU.logical_shift_right))
                link(nc.vector.tensor_tensor_scan(cum[:], ones1[:], tiles[:], 0.0, ALU.mult, ALU.add))
                link(nc.vector.tensor_tensor(first[:], cum[:], tiles[:], ALU.subtract))
                link(nc.vector.tensor_scalar(first[:], first[:], float(P), None, ALU.mult))
                link(nc.vector.tensor_tensor(posw[:], bank[4][:, 0:GE].rearrange("p (t e) -> p t e", t=GT),
                                             first[:, None, :].to_broadcast(all3), ALU.add))
                link(nc.vector.tensor_tensor(posw[:], posw[:], onehot[:], ALU.mult))
                link(nc.vector.tensor_reduce(posf[:], posw[:], X, ALU.add))
                nc.vector.tensor_copy(pos[g][:], posf[:]).then_inc(pos_ready, 1)
                tile3 = [1, GTILES, EXPERTS]
                link(nc.vector.tensor_tensor(over[:], cum[0:1, None, :].to_broadcast(tile3),
                                             cf[0:1, C_TILE:C_TILE + GTILES, None].to_broadcast(tile3), ALU.is_le))
                link(nc.vector.tensor_reduce(owner[:], over[:], X, ALU.add))
                nc.vector.tensor_scalar(expert[g][:], owner[:], float(EXPERTS - 1), None, ALU.min).then_inc(expert_ready, 1)

            def tables():
                for n, (tab, raw) in enumerate(((tabA, w1f), (tabB, w2f))):
                    v.wait_ge(hi_ready, n + 1)
                    nc.vector.scalar_tensor_tensor(out=tab[:, :, HIDDEN:2 * HIDDEN], in0=raw[:], scalar=WSCALE,
                                                   in1=tab[:, :, 0:HIDDEN], op0=ALU.mult, op1=ALU.subtract).then_inc(tables_ready, 1)
                v.wait_ge(bias_loaded, 16 * 6)
                link(nc.vector.tensor_scalar(bf[:], bf[:], WSCALE, None, ALU.mult))
                link(nc.vector.tensor_copy(bhi[:], bf[:]))
                link(nc.vector.scalar_tensor_tensor(out=bres[:], in0=bhi[:], scalar=cf[:, C_PART:C_PART + 1], in1=bf[:],
                                                    op0=ALU.mult, op1=ALU.add))
                link(nc.vector.tensor_copy(bhi[:], bres[:]))
                nc.vector.scalar_tensor_tensor(out=bres[:], in0=bhi[:], scalar=cf[:, C_PART + 1:C_PART + 2], in1=bres[:],
                                               op0=ALU.mult, op1=ALU.add).then_inc(tables_ready, 1)
                v.wait_ge(tables_ready, 3)
                for tab in (tabA, tabB):
                    nc.vector.tensor_copy(tab[:, :, 2 * HIDDEN:].bitcast(BF16), bres[:]).then_inc(tables_ready, 1)

            def act_split(f, i, s):
                n = f * NT + i * RING + s
                v.wait_ge(gelu_ready, n + 1)
                if not isinstance(i, int) or i > 0 or f > 0:
                    v.wait_ge(y_ready, n + (1 - RING))
                nc.vector.tensor_copy(acth[:, s, :], act[:, s, :]).then_inc(acth_ready, 1)
                v.wait_ge(acth_ready, n + 1)
                nc.vector.tensor_tensor(actl[:, s, :], act[:, s, :], acth[:, s, :], ALU.subtract).then_inc(actl_ready, 1)

            def y_copy(f, i, s):
                n = f * NT + i * RING + s
                v.wait_ge(y_ready, n + 1)
                if not isinstance(i, int) or i > 0:
                    v.wait_ge(y_stored[s], f * (16 * NT // RING) + i * 16)
                elif f > 0:
                    v.wait_ge(y_stored[s], 16 * NT // RING * f)
                nc.vector.tensor_scalar(ybuf[:, s, :], bank[3 + s][:, 0:D], 1.0 / WSCALE, None, ALU.mult).then_inc(y_copied, 1)

            def experts(f):
                for s in range(2):
                    act_split(f, 0, s)
                for s in range(RING):
                    act_split(f, *ahead(0, s, 2))
                    y_copy(f, 0, s)
                with v.Fori(1, NT // RING - 1) as i:
                    for s in range(RING):
                        act_split(f, *ahead(i, s, 2))
                        y_copy(f, i, s)
                act_split(f, NT // RING - 1, 2)
                for s in range(RING):
                    y_copy(f, NT // RING - 1, s)

            def add_ffn(f, g):
                for t in range(GT):
                    v.wait_ge(back_done[g][t], 16 * (f + 1))
                    last = nc.vector.scalar_tensor_tensor(out=x[:, g * GT + t, :], in0=yback[g][:, t, :], scalar=coef[g][:, t:t + 1],
                                                          in1=x[:, g * GT + t, :], op0=ALU.mult, op1=ALU.add)
                    if f == 1:
                        last.then_inc(x_final, 1)
                if f == 0:
                    link(last)

            def attend(g, h):
                a = 2 * g + h
                seq3 = [P, 2, SEQ]

                def table(c):
                    return cf[:, None, c:c + SEQ].to_broadcast(seq3)

                def two(ap):
                    return ap.rearrange("p (b s) -> p b s", b=2)

                v.wait_ge(q_ready, a + 1)
                if a:
                    v.wait_ge(att_ready, 2 * a)
                nc.vector.tensor_tensor(two(t1[:]), two(bank[0][:]), table(C_COST), ALU.mult)
                link(nc.vector.tensor_tensor(two(t2[:]), two(bank[1][:]), table(C_SINT), ALU.mult))
                nc.vector.tensor_tensor(qr[:], t1[:], t2[:], ALU.add).then_inc(qr_ready, 1)
                v.wait_ge(k_ready, a + 1)
                nc.vector.tensor_tensor(two(t3[:]), two(bank[4][:]), table(C_COSR), ALU.mult)
                link(nc.vector.tensor_tensor(two(t4[:]), two(bank[5][:]), table(C_SINR), ALU.mult))
                nc.vector.tensor_tensor(kr[:], t3[:], t4[:], ALU.add).then_inc(kr_ready, 1)
                v.wait_ge(vpad_ready, a + 1)
                link(nc.vector.tensor_scalar(local[:], vpad[:, :, 0:SEQ], lepe[:, 0:1], lepe[:, TAPS:TAPS + 1], ALU.mult, ALU.add))
                for k in range(1, TAPS):
                    link(nc.vector.scalar_tensor_tensor(out=local[:], in0=vpad[:, :, k:k + SEQ], scalar=lepe[:, k:k + 1],
                                                        in1=local[:], op0=ALU.mult, op1=ALU.add))
                v.wait_ge(kv_ready, a + 1)
                for b in range(2):
                    kv = bank[7][:, b * (P + 1):(b + 1) * (P + 1)]
                    nc.vector.tensor_tensor(kvm[:, b, :], kv[:, 0:P], mask, ALU.mult)
                    last = nc.vector.tensor_scalar(ksm[:, b, :], mask, kv[:, P:P + 1], None, ALU.mult)
                last.then_inc(kvm_ready, 1)
                for b in range(2):
                    v.wait_ge(den_copied, 2 * a + b + 1)
                    link(nc.vector.reciprocal(rden[:, b, :], den[:, b, :]))
                    nc.vector.scalar_tensor_tensor(out=att[:, b, :], in0=bank[4 + b][:, 0:SEQ], scalar=vsum[:, b:b + 1],
                                                   in1=rden[:, b, :], op0=ALU.add, op1=ALU.mult).then_inc(att_ready, 1)
                v.wait_ge(att_ready, 2 * a + 2)
                link(nc.vector.tensor_tensor(att[:], att[:], local[:], ALU.add))
                v.wait_ge(gate_copied, a + 1)
                nc.vector.tensor_tensor(two(gated[:]), att[:], two(gate[:]), ALU.mult).then_inc(gated_ready, 1)
                v.wait_ge(proj_ready, a + 1)
                rows = x[:, g * GT + 4 * h:g * GT + 4 * h + 4, :]
                nc.vector.tensor_tensor(rows, bank[6][:].rearrange("p (t c) -> p t c", t=4), rows, ALU.add).then_inc(x_updated, 1)

            v.wait_ge(consts_loaded, 16 * 4)
            v.wait_ge(pool_set, 1)
            for g in range(GROUPS):
                v.wait_ge(x_in_sem[g], 16)
                norm(NORM[0, g], g)
                split(NORM[0, g], 0, g)
                route(0, g)
            tables()
            experts(0)
            v.wait_ge(attn_loaded, 32)
            for g in range(GROUPS):
                add_ffn(0, g)
                norm(NORM["a", g], g)
                for h in range(2):
                    attend(g, h)
                v.wait_ge(x_updated, 2 * g + 2)
                norm(NORM[1, g], g)
                split(NORM[1, g], 1, g)
                route(1, g)
            experts(1)
            for g in range(GROUPS):
                add_ffn(1, g)

        @block.tensor
        def _(pe):
            def norm(k, g):
                for h in range(2):
                    pe.wait_ge(xn_ready, 2 * k + h + 1)
                    if k:
                        pe.wait_ge(xnT_ready, 2 * k)
                    for t in range(4):
                        last = nc.tensor.transpose(bank[6 + h][:, t * P:(t + 1) * P], xn[:, 4 * h + t, :], ident)
                    last.then_inc(xn_turned, 1)

            def route(k, f, g):
                n = GROUPS * f + g
                if n:
                    pe.wait_ge(pos_ready, n)
                for t in range(GT):
                    pe.wait_ge(xnT_ready, 2 * k + t // 4 + 1)
                    last = nc.tensor.matmul(bank[5][:, t * EXPERTS:(t + 1) * EXPERTS], xnT[g][:, t * P:(t + 1) * P], wr[:],
                                            start=True, stop=True)
                last.then_inc(logits_ready, 1)
                pe.wait_ge(onehot_ready, n + 1)
                hot = onehot[:].rearrange("p t e -> p (t e)")
                nc.tensor.matmul(bank[4][:, 0:GE], before, hot, start=True, stop=False, skip_group_check=True)
                for d in range(1, GT):
                    nc.tensor.matmul(bank[4][:, d * EXPERTS:GE], ones16, hot[:, 0:GE - d * EXPERTS], start=False, stop=False,
                                     skip_group_check=True)
                for t in range(GT):
                    last = nc.tensor.matmul(bank[4][:, GE:GE + EXPERTS], ones16, onehot[:, t, :], start=False,
                                            stop=(t == GT - 1), skip_group_check=True)
                last.then_inc(ranks_ready, 1)

            def turn(f, i, s):
                n = f * NT + i * RING + s
                pe.wait_ge(x_landed[s], f * (16 * NT // RING) + i * 16 + 16)
                if not isinstance(n, int) or n > 0:
                    pe.wait_ge(tileT_ready, n)
                xt = bank[6 + s % 2][:, 0:P].bitcast(F16)
                for k in range(2):
                    last = nc.tensor.transpose(xt[:, k * P:(k + 1) * P], ringX[:, s, k * D:(k + 1) * D], ident16)
                last.then_inc(tile_turned, 1)

            def hidden(f, i, s):
                n = f * NT + i * RING + s
                pe.wait_ge(a_landed[s], f * (16 * NT // RING) + i * 16 + 16)
                pe.wait_ge(tileT_ready, n + 1)
                if not isinstance(i, int) or i > 0 or f > 0:
                    pe.wait_ge(gelu_ready, n + (1 - RING))
                hb, w = bank[s], ringA[:, s, :]
                xh, xl = ringT[:, s, 0:P], ringT[:, s, P:2 * P]
                nc.tensor.matmul(hb[:], w[:, 2 * HIDDEN:].bitcast(BF16), chunk_sel, start=True, stop=False, skip_group_check=True)
                for c in range(HC):
                    o = hb[:, c * P:(c + 1) * P]
                    hi, lo = w[:, c * P:(c + 1) * P], w[:, HIDDEN + c * P:HIDDEN + (c + 1) * P]
                    nc.tensor.matmul(o, hi, xh, start=False, stop=False, skip_group_check=True)
                    nc.tensor.matmul(o, hi, xl, start=False, stop=False, skip_group_check=True)
                    last = nc.tensor.matmul(o, lo, xh, start=False, stop=(c == HC - 1), skip_group_check=True)
                last.then_inc(hid_ready, 1)

            def project(f, i, s):
                n = f * NT + i * RING + s
                pe.wait_ge(b_landed[s], f * (16 * NT // RING) + i * 16 + 16)
                pe.wait_ge(actl_ready, n + 1)
                if not isinstance(i, int) or i > 0 or f > 0:
                    pe.wait_ge(y_copied, n + (1 - RING))
                o, w = bank[3 + s][:, 0:D], ringB[:, s, :]
                nc.tensor.matmul(o, ones16[96:99, :], w[96:99, 2 * HIDDEN:].bitcast(BF16), start=True, stop=False)
                for c in range(HC):
                    hi, lo = w[:, c * P:(c + 1) * P], w[:, HIDDEN + c * P:HIDDEN + (c + 1) * P]
                    ah, al = acth[:, s, c * P:(c + 1) * P], actl[:, s, c * P:(c + 1) * P]
                    nc.tensor.matmul(o, ah, hi, start=False, stop=False)
                    nc.tensor.matmul(o, ah, lo, start=False, stop=False)
                    last = nc.tensor.matmul(o, al, hi, start=False, stop=(c == HC - 1))
                last.then_inc(y_ready, 1)

            def experts(f):
                for s in range(RING):
                    turn(f, 0, s)
                for s in range(2):
                    hidden(f, 0, s)
                pe.wait_ge(pos_ready, GROUPS * (f + 1))
                for s in range(RING):
                    turn(f, 1, s)
                    hidden(f, *ahead(0, s, 2))
                    project(f, 0, s)
                with pe.Fori(1, NT // RING - 1) as i:
                    for s in range(RING):
                        turn(f, i + 1, s)
                        hidden(f, *ahead(i, s, 2))
                        project(f, i, s)
                hidden(f, NT // RING - 1, 2)
                for s in range(RING):
                    project(f, NT // RING - 1, s)

            def attend(g, h):
                a = 2 * g + h
                xt = xnT[g][:, h * HALF:(h + 1) * HALF]
                if a:
                    pe.wait_ge(qr_ready, a)
                    pe.wait_ge(vpad_ready, a)
                    pe.wait_ge(gate_copied, a)
                    pe.wait_ge(att_ready, 2 * a)
                    pe.wait_ge(x_updated, a)
                nc.tensor.matmul(bank[0][:], wattn[:, 0, :], xt, start=True, stop=True)
                nc.tensor.matmul(bank[1][:], wattn[:, 1, :], xt, start=True, stop=True).then_inc(q_ready, 1)
                nc.tensor.matmul(bank[2][:], wattn[:, 2, :], xt, start=True, stop=True).then_inc(v_ready, 1)
                nc.tensor.matmul(bank[3][:], wattn[:, 3, :], xt, start=True, stop=True).then_inc(gate_ready, 1)
                for w, b, done in ((4, 4, None), (5, 5, k_ready), (2, 6, vrow_ready)):
                    for t in range(4):
                        last = nc.tensor.matmul(bank[b][:, t * P:(t + 1) * P], xt[:, t * P:(t + 1) * P], wattn[:, w, :],
                                                start=True, stop=True)
                    if done:
                        last.then_inc(done, 1)
                pe.wait_ge(kr_ready, a + 1)
                pe.wait_ge(vrow_copied, a + 1)
                for b in range(2):
                    for t in range(2):
                        last = nc.tensor.matmul(bank[7][:, b * (P + 1):(b + 1) * (P + 1)], kr[:, (2 * b + t) * P:(2 * b + t + 1) * P],
                                                vrow[:, 2 * b + t, :], start=(t == 0), stop=(t == 1))
                last.then_inc(kv_ready, 1)
                pe.wait_ge(kvm_ready, a + 1)
                pe.wait_ge(qr_ready, a + 1)
                for b in range(2):
                    q = qr[:, b * SEQ:(b + 1) * SEQ]
                    nc.tensor.matmul(bank[4 + b][:, 0:SEQ], kvm[:, b, :], q, start=True, stop=True)
                    nc.tensor.matmul(bank[4 + b][:, SEQ:2 * SEQ], ksm[:, b, :], q, start=True, stop=True).then_inc(nd_ready, 1)
                pe.wait_ge(gated_ready, a + 1)
                for t in range(4):
                    last = nc.tensor.matmul(bank[6][:, t * P:(t + 1) * P], gated[:, t * P:(t + 1) * P], wattn[:, 6, :],
                                            start=True, stop=True)
                last.then_inc(proj_ready, 1)

            pe.wait_ge(consts_loaded, 16 * 4)
            for g in range(GROUPS):
                norm(NORM[0, g], g)
                route(NORM[0, g], 0, g)
            experts(0)
            pe.wait_ge(attn_loaded, 32)
            pe.wait_ge(y_copied, NT)
            for g in range(GROUPS):
                norm(NORM["a", g], g)
                pe.wait_ge(xnT_ready, 2 * NORM["a", g] + 2)
                if g:
                    pe.wait_ge(pos_ready, GROUPS + g)
                for h in range(2):
                    attend(g, h)
                norm(NORM[1, g], g)
                route(NORM[1, g], 1, g)
            experts(1)


def kernel(**inputs):
    import concourse.bacc as bacc
    from concourse.bass_utils import run_bass_kernel_spmd

    def arr(name):
        return np.ascontiguousarray(inputs[name])

    def turned(name):
        return np.asarray(inputs[name]).T

    swap = (np.arange(P) // DK) * DK + (np.arange(P) + DK // 2) % DK
    q, k = turned("L0_attn_Wq"), turned("L0_attn_Wk")
    wattn = np.stack([q, q[:, swap], turned("L0_attn_Wv"), turned("L0_attn_Wg"), k, k[:, swap], turned("L0_attn_Wo")], axis=1)
    lepe = np.concatenate([arr("L0_attn_lepe_w").reshape(D, TAPS), arr("L0_attn_lepe_b").reshape(D, 1)], axis=1)
    cf, ch = constants()
    arrays = {
        "x_in": arr("L0_attn_hidden_states").reshape(TOKENS, D),
        "wr_in": arr("L0_ffn_Wr"), "br_in": arr("L0_ffn_br").reshape(1, EXPERTS),
        "w1_in": arr("L0_ffn_W1"), "b1_in": arr("L0_ffn_b1"), "w2_in": arr("L0_ffn_W2"), "b2_in": arr("L0_ffn_b2"),
        "wattn_in": np.ascontiguousarray(wattn), "lepe_in": np.ascontiguousarray(lepe), "cf_in": cf, "ch_in": ch,
    }
    nc = bacc.Bacc("TRN2", target_bir_lowering=False, num_devices=1)
    args = [nc.dram_tensor(n, a.shape, mybir.dt.from_np(a.dtype), kind="ExternalInput").ap() for n, a in arrays.items()]
    out = nc.dram_tensor("out", [TOKENS, D], F32, kind="ExternalOutput").ap()
    program(nc, *args, out)
    r = run_bass_kernel_spmd(nc, [arrays], core_ids=[0])
    return r.results[0]["out"].reshape(TOKENS // SEQ, SEQ, D)
```

```python
from contextlib import ExitStack

import numpy as np

import concourse.bass as bass
from concourse import mybir

P = 128
D = 128
TOKENS, SEQ = 2048, 256
HEADS, DK = 8, 16
EXPERTS, HIDDEN = 8, 512
HC = HIDDEN // P
GROUPS = 2
GT = TOKENS // GROUPS // P
GE = GT * EXPERTS
GTILES = (TOKENS // GROUPS - EXPERTS) // P + EXPERTS
NT = GROUPS * GTILES
SLOTS = NT * P
RING = 3
TURN = 6
TURNS = NT // TURN
HALF = 512
TAPS = 5
EPS = 1e-5
WSCALE = 64.0
WCOLS = 4 * HIDDEN

F32, F16, BF16 = mybir.dt.float32, mybir.dt.float16, mybir.dt.bfloat16
I32, U32 = mybir.dt.int32, mybir.dt.uint32
ALU = mybir.AluOpType
ACT = mybir.ActivationFunctionType
X = mybir.AxisListType.X

C_ID, C_MASK, C_COST, C_SINT = 0, 128, 256, 512
C_COSR, C_SINR, C_RANK, C_TILE, C_PART, C_END = 768, 1024, 1280, 1288, 1288 + GTILES, 1291 + GTILES


def constants():
    f = np.zeros((P, C_END), np.float32)
    f[:, C_ID:C_ID + P] = np.eye(P)
    head = np.arange(P) // DK
    f[:, C_MASK:C_MASK + P] = (head[:, None] == head[None, :]) * np.float32(DK ** -0.5)
    inv = (1.0 / np.float32(10000.0) ** (np.arange(0, DK, 2, dtype=np.float32) / np.float32(DK))).astype(np.float32)
    ang = np.arange(SEQ, dtype=np.float32)[:, None] * inv[None, :]
    ang = np.tile(np.concatenate([ang, ang], axis=1), (1, HEADS))
    sign = np.where(np.arange(P) % DK < DK // 2, -1.0, 1.0).astype(np.float32)
    cos, sin = np.cos(ang).astype(np.float32), np.sin(ang).astype(np.float32) * sign[None, :]
    f[:, C_COST:C_COST + SEQ], f[:, C_SINT:C_SINT + SEQ] = cos.T, sin.T
    f[:, C_COSR:C_COSR + SEQ] = cos.reshape(2, P, P).transpose(1, 0, 2).reshape(P, SEQ)
    f[:, C_SINR:C_SINR + SEQ] = sin.reshape(2, P, P).transpose(1, 0, 2).reshape(P, SEQ)
    f[:, C_RANK:C_RANK + EXPERTS] = EXPERTS - np.arange(EXPERTS)
    f[:, C_TILE:C_TILE + GTILES] = np.arange(GTILES)
    part, expert = np.arange(P) // EXPERTS, np.arange(P) % EXPERTS
    f[:, C_PART] = -(part >= 1).astype(np.float32)
    f[:, C_PART + 1] = -(part >= 2).astype(np.float32)
    f[:, C_PART + 2] = np.where(part < 3, expert, -1)
    h = np.zeros((P, 3 * P), np.float16)
    h[:, 0:P] = np.eye(P)
    h[:, P:2 * P] = np.triu(np.ones((P, P)), 1)
    h[:, 2 * P:3 * P] = 1
    return f, h


def program(nc, x_in, wr_in, br_in, w1_in, b1_in, w2_in, b2_in, wattn_in, lepe_in, cf_in, ch_in, out):
    with ExitStack() as ctx:
        def sb(name, shape, dt=F32):
            return ctx.enter_context(nc.sbuf_tensor(name, shape, dt))

        def sem(name):
            return ctx.enter_context(nc.semaphore(name))

        sorted_x = nc.dram_tensor("sorted_x", [SLOTS, 2 * D], F16, kind="Internal").ap()
        sorted_y = nc.dram_tensor("sorted_y", [SLOTS, D], F32, kind="Internal").ap()

        bank = [ctx.enter_context(nc.psum_tensor(f"bank{i}", [P, 512], F32)) for i in range(8)]

        cf, ch = sb("cf", [P, C_END]), sb("ch", [P, 3 * P], F16)
        ident, mask = cf[:, C_ID:C_ID + P], cf[:, C_MASK:C_MASK + P]
        rank = cf[:, C_RANK:C_RANK + EXPERTS]
        ident16, before, ones16 = ch[:, 0:P], ch[:, P:2 * P], ch[:, 2 * P:3 * P]
        x = sb("x", [P, GROUPS * GT, D])
        wr, br = sb("wr", [P, EXPERTS]), sb("br", [P, EXPERTS])
        wattn = sb("wattn", [P, 7, P])
        lepe = sb("lepe", [P, TAPS + 1])
        w1f, w2f = sb("w1f", [P, EXPERTS, HIDDEN]), sb("w2f", [P, EXPERTS, HIDDEN])
        bf, bres = sb("bf", [P, HC + 1, P]), sb("bres", [P, HC + 1, P])
        bhi, bias = sb("bhi", [P, HC + 1, P], BF16), sb("bias", [P, HC + 1, P], BF16)
        table = sb("table", [P, EXPERTS, WCOLS], F16)
        zeros = sb("zeros", [P, 2 * D], F16)

        bn, mv = sb("bn", [P, GT, 6]), sb("mv", [P, GT, 2])
        std, rstd, eps = sb("std", [P, GT]), sb("rstd", [P, GT]), sb("eps", [P, 1])
        xn = sb("xn", [P, GT, D])
        xs = [sb(f"xs{g}", [P, GT, 2 * D], F16) for g in range(GROUPS)]
        xnT = [sb(f"xnT{g}", [P, GT * P]) for g in range(GROUPS)]
        lg, top, ld = sb("lg", [P, GT, EXPERTS]), sb("top", [P, GT]), sb("ld", [P, GT, EXPERTS])
        score, best = sb("score", [P, GT, EXPERTS]), sb("best", [P, GT])
        onehot = sb("onehot", [P, GT, EXPERTS], F16)
        ex, exsum = sb("ex", [P, GT, EXPERTS]), sb("exsum", [P, GT])
        coef = [sb(f"coef{g}", [P, GT]) for g in range(GROUPS)]
        cnt, tiles = sb("cnt", [P, EXPERTS], I32), sb("tiles", [P, EXPERTS], I32)
        cum, first = sb("cum", [P, EXPERTS]), sb("first", [P, EXPERTS])
        posw, posf = sb("posw", [P, GT, EXPERTS]), sb("posf", [P, GT])
        pos = [sb(f"pos{g}", [P, GT], U32) for g in range(GROUPS)]
        over, owner = sb("over", [P, GTILES, EXPERTS]), sb("owner", [P, GTILES])
        expert = sb("expert", [P, NT], I32)
        isrow = sb("isrow", [P, NT], F16)
        rowsel = sb("rowsel", [P, NT, P], F16)
        ones1 = sb("ones1", [P, EXPERTS])

        ringW = sb("ringW", [P, TURN, WCOLS], F16)
        ringX, ringT = sb("ringX", [P, TURN, 2 * D], F16), sb("ringT", [P, RING, 2 * P], F16)
        act = sb("act", [P, RING, HIDDEN])
        acth, actl = sb("acth", [P, RING, HIDDEN], F16), sb("actl", [P, RING, HIDDEN], F16)
        ybuf = sb("ybuf", [P, TURN, D])
        yback = [sb(f"yback{g}", [P, GT, D]) for g in range(GROUPS)]

        t1, t2, t3, t4 = (sb(f"t{i}", [P, HALF]) for i in range(4))
        qr, kr = sb("qr", [P, HALF]), sb("kr", [P, HALF])
        vpad, vsum = sb("vpad", [P, 2, SEQ + TAPS - 1]), sb("vsum", [P, 2])
        gate = sb("gate", [P, HALF])
        vrow = sb("vrow", [P, 4, P + 1])
        kvm, ksm = sb("kvm", [P, 2, P]), sb("ksm", [P, 2, P])
        den, rden = sb("den", [P, 2, SEQ]), sb("rden", [P, 2, SEQ])
        local, att = sb("local", [P, 2, SEQ]), sb("att", [P, 2, SEQ])
        gated = sb("gated", [P, HALF])
        seqlen = sb("seqlen", [P, 1])

        x_in_sem = [sem(f"x_loaded{g}") for g in range(GROUPS)]
        consts_loaded, attn_loaded, w1_loaded, w2_loaded = (
            sem(n) for n in ("consts_loaded", "attn_loaded", "w1_loaded", "w2_loaded"))
        bias_zeroed, bias_loaded = sem("bias_zeroed"), sem("bias_loaded")
        zeros_set, slots_cleared, pool_set = sem("zeros_set"), sem("slots_cleared"), sem("pool_set")
        w1_high, w2_scaled, w2_high = sem("w1_high"), sem("w2_scaled"), sem("w2_high")
        w1_low, w2_low, bias_ready = sem("w1_low"), sem("w2_low"), sem("bias_ready")
        stats_ready, std_ready, xn_ready = sem("stats_ready"), sem("std_ready"), sem("xn_ready")
        xn_turned, xnT_ready = sem("xn_turned"), sem("xnT_ready")
        logits_ready, shifted_ready, exp_ready = sem("logits_ready"), sem("shifted_ready"), sem("exp_ready")
        onehot_ready, ranks_ready = sem("onehot_ready"), sem("ranks_ready")
        pos_ready, expert_ready, xs_ready = sem("pos_ready"), sem("expert_ready"), sem("xs_ready")
        isrow_ready, rowsel_ready = sem("isrow_ready"), sem("rowsel_ready")
        sorted_done = [sem(f"sorted_done{g}") for g in range(GROUPS)]
        back_done = [[sem(f"back_done{g}_{t}") for t in range(GT)] for g in range(GROUPS)]
        w_landed = [sem(f"w_landed{s}") for s in range(TURN)]
        x_landed = [sem(f"x_landed{q}") for q in range(2)]
        y_stored = [sem(f"y_stored{q}") for q in range(2)]
        tile_turned, tileT_ready = sem("tile_turned"), sem("tileT_ready")
        hid_ready, gelu_ready = sem("hid_ready"), sem("gelu_ready")
        acth_ready, actl_ready = sem("acth_ready"), sem("actl_ready")
        y_ready, y_copied = sem("y_ready"), sem("y_copied")
        q_ready, v_ready, gate_ready, k_ready, vrow_ready = (
            sem(n) for n in ("q_ready", "v_ready", "gate_ready", "k_ready", "vrow_ready"))
        qr_ready, kr_ready, vpad_ready, gate_copied, vrow_copied = (
            sem(n) for n in ("qr_ready", "kr_ready", "vpad_ready", "gate_copied", "vrow_copied"))
        kv_ready, kvm_ready, nd_ready, den_copied, att_ready = (
            sem(n) for n in ("kv_ready", "kvm_ready", "nd_ready", "den_copied", "att_ready"))
        gated_ready, proj_ready, x_updated = sem("gated_ready"), sem("proj_ready"), sem("x_updated")
        x_final, stored = sem("x_final"), sem("stored")
        dve_step, pool_step = sem("dve_step"), sem("pool_step")

        NORM = {(0, 0): 0, (0, 1): 1, ("a", 0): 2, (1, 0): 3, ("a", 1): 4, (1, 1): 5}

        def ahead(i, s, d):
            return i + (s + d) // TURN, (s + d) % TURN

        def later(f, i):
            return f > 0 or not isinstance(i, int) or i > 0

        block = ctx.enter_context(nc.Block())

        @block.sync
        def _(sp):
            def load_rows(g):
                sp.dma_start(x[:, g * GT:(g + 1) * GT, :],
                             x_in[g * GT * P:(g + 1) * GT * P, :].rearrange("(t p) d -> p t d", p=P)
                             ).then_inc(x_in_sem[g], 16)

            load_rows(0)
            sp.dma_start(cf[:], cf_in).then_inc(consts_loaded, 16)
            sp.dma_start(ch[:], ch_in).then_inc(consts_loaded, 16)
            sp.dma_start(wr[:], wr_in).then_inc(consts_loaded, 16)
            sp.dma_start(br[:], br_in.to_broadcast([P, EXPERTS])).then_inc(consts_loaded, 16)
            load_rows(1)
            sp.wait_ge(zeros_set, 1)
            sp.dma_start(sorted_x.rearrange("(n p) d -> p n d", p=P),
                         zeros[:, None, :].to_broadcast([P, NT, 2 * D])).then_inc(slots_cleared, 16)
            sp.dma_start(w1f[:], w1_in.rearrange("e d h -> d e h")).then_inc(w1_loaded, 16)
            sp.dma_start(w2f[:].rearrange("p e (c d) -> p e c d", c=HC),
                         w2_in.rearrange("e (c p) d -> p e c d", p=P)).then_inc(w2_loaded, 16)
            sp.wait_ge(bias_zeroed, 1)
            for k in range(3):
                rows = slice(EXPERTS * k, EXPERTS * (k + 1))
                sp.dma_start(bf[rows, 0:HC, :], b1_in.rearrange("e (c p) -> e c p", p=P)).then_inc(bias_loaded, 16)
                sp.dma_start(bf[rows, HC, :], b2_in).then_inc(bias_loaded, 16)
            sp.dma_start(wattn[:], wattn_in).then_inc(attn_loaded, 16)
            sp.dma_start(lepe[:], lepe_in).then_inc(attn_loaded, 16)

            def load_tile_rows(f, i, q):
                if later(f, i):
                    sp.wait_ge(tile_turned, f * NT + i * TURN + (q * RING + RING - TURN))
                row = i * (TURN * P) + q * RING * P
                sp.dma_start(ringX[:, q * RING:(q + 1) * RING, :],
                             sorted_x[bass.ds(row, RING * P), :].rearrange("(t p) d -> p t d", p=P)).then_inc(x_landed[q], 16)

            def load_weights(f, i, s):
                tile = i * TURN + s
                e = sp.value_load(expert[0:1, bass.ds(tile, 1)], min_val=0, max_val=EXPERTS - 1)
                if later(f, i):
                    sp.wait_ge(y_ready, f * NT + i * TURN + (s + 1 - TURN))
                sp.dma_start(ringW[:, s, :], table[:, bass.ds(e, 1), :]).then_inc(w_landed[s], 16)

            def turn(f, i):
                for s in range(TURN):
                    if s % RING == 0:
                        load_tile_rows(f, i, s // RING)
                    load_weights(f, i, s)

            sp.wait_ge(w1_low, 1)
            sp.wait_ge(w2_low, 1)
            for f in range(2):
                sp.wait_ge(expert_ready, GROUPS * f + 1)
                sp.wait_ge(sorted_done[0], 16 * GT * (f + 1))
                turn(f, 0)
                turn(f, 1)
                sp.wait_ge(expert_ready, GROUPS * f + 2)
                sp.wait_ge(sorted_done[1], 16 * GT * (f + 1))
                with sp.Fori(2, TURNS) as i:
                    turn(f, i)
            for g in range(GROUPS):
                for t in range(0, GT, 2):
                    n = g * GT + t
                    sp.wait_ge(x_final, n + 2)
                    sp.dma_start(out[n * P:(n + 2) * P, :].rearrange("(t p) d -> p t d", p=P),
                                 x[:, n:n + 2, :]).then_inc(stored, 16)
            sp.wait_ge(stored, 16 * GROUPS * GT // 2)

        @block.gpsimd
        def _(pool):
            nc.gpsimd.memset(bf[:], 0.0).then_inc(bias_zeroed, 1)
            nc.gpsimd.memset(zeros[:], 0.0).then_inc(zeros_set, 1)
            nc.gpsimd.memset(vpad[:], 0.0)
            nc.gpsimd.memset(ones1[:], 1.0)
            nc.gpsimd.memset(eps[:], EPS)
            nc.gpsimd.memset(seqlen[:], float(SEQ))
            nc.gpsimd.memset(vrow[:], 1.0).then_inc(pool_set, 1)

            def sort_out(f, g):
                pool.wait_ge(xs_ready, GROUPS * f + g + 1)
                pool.wait_ge(pos_ready, GROUPS * f + g + 1)
                for t in range(GT):
                    nc.gpsimd.indirect_dma_start(
                        out=sorted_x, out_offset=bass.IndirectOffsetOnAxis(ap=pos[g][:, t:t + 1], axis=0),
                        in_=xs[g][:, t, :], in_offset=None).then_inc(sorted_done[g], 16)
                pool.wait_ge(isrow_ready, GROUPS * f + g + 1)
                own = slice(g * GTILES, (g + 1) * GTILES)
                if f:
                    pool.wait_ge(y_ready, NT)
                nc.gpsimd.tensor_copy(rowsel[:, own, :], isrow[:, own, None].to_broadcast([P, GTILES, P])).then_inc(rowsel_ready, 1)

            def sort_back(f, g):
                tiles_before = f * NT + (g + 1) * GTILES
                for q in range(2):
                    pool.wait_ge(y_stored[q], 16 * ((tiles_before // RING + 1 - q) // 2))
                for t in range(GT):
                    nc.gpsimd.indirect_dma_start(
                        out=yback[g][:, t, :], out_offset=None, in_=sorted_y[0:(g + 1) * GTILES * P, :],
                        in_offset=bass.IndirectOffsetOnAxis(ap=pos[g][:, t:t + 1], axis=0)).then_inc(back_done[g][t], 16)

            pool.wait_ge(w2_high, 1)
            nc.gpsimd.tensor_tensor(table[:, :, 3 * HIDDEN:], w2f[:], table[:, :, 2 * HIDDEN:3 * HIDDEN],
                                    ALU.subtract).then_inc(w2_low, 1)
            pool.wait_ge(slots_cleared, 16)
            for f in range(2):
                for g in range(GROUPS):
                    sort_out(f, g)
                for g in range(GROUPS):
                    sort_back(f, g)

        @block.scalar
        def _(sc):
            def norm(k, g):
                sc.wait_ge(stats_ready, k + 1)
                nc.scalar.activation(std[:], mv[:, :, 1], ACT.Sqrt, bias=eps[:]).then_inc(std_ready, 1)
                for h in range(2):
                    sc.wait_ge(xn_turned, 2 * k + h + 1)
                    nc.scalar.copy(xnT[g][:, h * HALF:(h + 1) * HALF], bank[6 + h][:]).then_inc(xnT_ready, 1)

            def route(f, g):
                sc.wait_ge(shifted_ready, GROUPS * f + g + 1)
                nc.scalar.activation(ex[:], ld[:], ACT.Exp).then_inc(exp_ready, 1)

            def turn_copy(f, i, s):
                n = f * NT + i * TURN + s
                sc.wait_ge(tile_turned, n + 1)
                if later(f, i) or s >= RING:
                    sc.wait_ge(hid_ready, n + (1 - RING))
                nc.scalar.copy(ringT[:, s % RING, :], bank[6 + s % 2][:, 0:P].bitcast(F16)).then_inc(tileT_ready, 1)

            def gelu(f, i, s):
                n = f * NT + i * TURN + s
                sc.wait_ge(hid_ready, n + 1)
                if later(f, i) or s >= RING:
                    sc.wait_ge(actl_ready, n + (1 - RING))
                nc.scalar.activation(act[:, s % RING, :], bank[s % RING][:], ACT.Gelu, scale=1.0 / WSCALE).then_inc(gelu_ready, 1)

            def y_copy(f, i, s):
                q = s // RING
                sc.wait_ge(y_ready, f * NT + i * TURN + s + 1)
                if s % RING == 0 and later(f, i):
                    sc.wait_ge(y_stored[q], f * (16 * TURNS) + i * 16)
                nc.scalar.activation(ybuf[:, s, :], bank[3 + s % RING][:, 0:D], ACT.Copy, scale=1.0 / WSCALE).then_inc(y_copied, 1)
                if s % RING == RING - 1:
                    sc.wait_ge(y_copied, f * NT + i * TURN + s + 1)
                    row = i * (TURN * P) + q * RING * P
                    sc.dma_start(sorted_y[bass.ds(row, RING * P), :].rearrange("(t p) d -> p t d", p=P),
                                 ybuf[:, q * RING:(q + 1) * RING, :]).then_inc(y_stored[q], 16)

            def step(f, i, s, first=False, last=False):
                if not last or s + 3 < TURN:
                    turn_copy(f, *ahead(i, s, 3))
                if not first or s:
                    y_copy(f, *ahead(i, s, -1))
                if not last or s + 2 < TURN:
                    gelu(f, *ahead(i, s, 2))

            def experts(f):
                for s in range(3):
                    turn_copy(f, 0, s)
                for s in range(2):
                    gelu(f, 0, s)
                for s in range(TURN):
                    step(f, 0, s, first=True)
                with sc.Fori(1, TURNS - 1) as i:
                    for s in range(TURN):
                        step(f, i, s)
                for s in range(TURN):
                    step(f, TURNS - 1, s, last=True)
                y_copy(f, TURNS - 1, TURN - 1)

            def attend(g, h):
                a = 2 * g + h
                sc.wait_ge(v_ready, a + 1)
                for b in range(2):
                    last = nc.scalar.activation(vpad[:, b, 2:2 + SEQ], bank[2][:, b * SEQ:(b + 1) * SEQ], ACT.Copy,
                                                accum_out=vsum[:, b:b + 1])
                last.then_inc(vpad_ready, 1)
                sc.wait_ge(gate_ready, a + 1)
                nc.scalar.copy(gate[:], bank[3][:]).then_inc(gate_copied, 1)
                sc.wait_ge(vrow_ready, a + 1)
                nc.scalar.copy(vrow[:, :, 0:P], bank[6][:].rearrange("p (t c) -> p t c", t=4)).then_inc(vrow_copied, 1)
                for b in range(2):
                    sc.wait_ge(nd_ready, 2 * a + b + 1)
                    nc.scalar.activation(den[:, b, :], bank[4 + b][:, SEQ:2 * SEQ], ACT.Identity,
                                         bias=seqlen[:]).then_inc(den_copied, 1)

            sc.wait_ge(pool_set, 1)
            norm(0, 0)
            route(0, 0)
            sc.wait_ge(w1_loaded, 16)
            nc.scalar.activation(table[:, :, 0:HIDDEN], w1f[:], ACT.Copy, scale=WSCALE).then_inc(w1_high, 1)
            sc.wait_ge(w2_loaded, 16)
            nc.scalar.activation(w2f[:], w2f[:], ACT.Copy, scale=WSCALE).then_inc(w2_scaled, 1)
            sc.wait_ge(w2_scaled, 1)
            nc.scalar.copy(table[:, :, 2 * HIDDEN:3 * HIDDEN], w2f[:]).then_inc(w2_high, 1)
            norm(1, 1)
            route(0, 1)
            experts(0)
            for g in range(GROUPS):
                norm(NORM["a", g], g)
                for h in range(2):
                    attend(g, h)
                norm(NORM[1, g], g)
                route(1, g)
            experts(1)

        @block.vector
        def _(v):
            steps = [0]

            def link(ins):
                steps[0] += 1
                ins.then_inc(dve_step, 1)
                v.wait_ge(dve_step, steps[0])

            def norm(k, g):
                for t in range(GT):
                    last = nc.vector.bn_stats(bn[:, t, :], x[:, g * GT + t, :])
                link(last)
                for t in range(GT):
                    last = nc.vector.bn_aggr(mv[:, t, :], bn[:, t, :])
                last.then_inc(stats_ready, 1)
                v.wait_ge(std_ready, k + 1)
                if k:
                    v.wait_ge(xn_turned, 2 * k)
                link(nc.vector.reciprocal(rstd[:], std[:]))
                for t in range(GT):
                    last = nc.vector.tensor_scalar(xn[:, t, :], x[:, g * GT + t, :], mv[:, t, 0:1], rstd[:, t:t + 1],
                                                   ALU.subtract, ALU.mult)
                    if t % 4 == 3:
                        last.then_inc(xn_ready, 1)

            def split(k, f, g):
                v.wait_ge(xn_ready, 2 * k + 2)
                link(nc.vector.tensor_copy(xs[g][:, :, 0:D], xn[:]))
                nc.vector.tensor_tensor(xs[g][:, :, D:2 * D], xn[:], xs[g][:, :, 0:D], ALU.subtract).then_inc(xs_ready, 1)

            def route(f, g):
                n = GROUPS * f + g
                v.wait_ge(logits_ready, n + 1)
                all3 = [P, GT, EXPERTS]
                link(nc.vector.tensor_tensor(lg[:], bank[5][:, 0:GE].rearrange("p (t e) -> p t e", t=GT),
                                             br[:, None, :].to_broadcast(all3), ALU.add))
                link(nc.vector.tensor_reduce(top[:], lg[:], X, ALU.max))
                nc.vector.tensor_tensor(ld[:], lg[:], top[:, :, None].to_broadcast(all3), ALU.subtract).then_inc(shifted_ready, 1)
                v.wait_ge(shifted_ready, n + 1)
                link(nc.vector.scalar_tensor_tensor(out=score[:], in0=ld[:], scalar=0.0, in1=rank[:, None, :].to_broadcast(all3),
                                                    op0=ALU.is_ge, op1=ALU.mult))
                link(nc.vector.tensor_reduce(best[:], score[:], X, ALU.max))
                nc.vector.tensor_tensor(onehot[:], score[:], best[:, :, None].to_broadcast(all3), ALU.is_equal).then_inc(onehot_ready, 1)
                v.wait_ge(exp_ready, n + 1)
                link(nc.vector.tensor_reduce(exsum[:], ex[:], X, ALU.add))
                link(nc.vector.reciprocal(best[:], exsum[:]))
                link(nc.vector.tensor_scalar(coef[g][:], best[:], 0.5, None, ALU.mult))
                v.wait_ge(ranks_ready, n + 1)
                link(nc.vector.tensor_scalar(cnt[:], bank[4][:, GE:GE + EXPERTS], float(P - 1), None, ALU.add))
                link(nc.vector.tensor_scalar(tiles[:], cnt[:], P.bit_length() - 1, None, ALU.logical_shift_right))
                link(nc.vector.tensor_tensor_scan(cum[:], ones1[:], tiles[:], 0.0, ALU.mult, ALU.add))
                link(nc.vector.tensor_tensor(first[:], cum[:], tiles[:], ALU.subtract))
                link(nc.vector.tensor_scalar(first[:], first[:], float(P), float(g * GTILES * P), ALU.mult, ALU.add))
                link(nc.vector.tensor_tensor(posw[:], bank[4][:, 0:GE].rearrange("p (t e) -> p t e", t=GT),
                                             first[:, None, :].to_broadcast(all3), ALU.add))
                link(nc.vector.tensor_tensor(posw[:], posw[:], onehot[:], ALU.mult))
                link(nc.vector.tensor_reduce(posf[:], posw[:], X, ALU.add))
                nc.vector.tensor_copy(pos[g][:], posf[:]).then_inc(pos_ready, 1)
                own, tile3 = slice(g * GTILES, (g + 1) * GTILES), [P, GTILES, EXPERTS]
                link(nc.vector.tensor_tensor(over[:], cum[:, None, :].to_broadcast(tile3),
                                             cf[:, C_TILE:C_TILE + GTILES, None].to_broadcast(tile3), ALU.is_le))
                link(nc.vector.tensor_reduce(owner[:], over[:], X, ALU.add))
                nc.vector.tensor_scalar(expert[:, own], owner[:], float(EXPERTS - 1), None, ALU.min).then_inc(expert_ready, 1)
                nc.vector.tensor_scalar(isrow[:, own], owner[:], float(EXPERTS - 1), cf[:, C_PART + 2:C_PART + 3],
                                        ALU.min, ALU.is_equal).then_inc(isrow_ready, 1)

            def tables():
                v.wait_ge(w1_high, 1)
                nc.vector.scalar_tensor_tensor(out=table[:, :, HIDDEN:2 * HIDDEN], in0=w1f[:], scalar=WSCALE,
                                               in1=table[:, :, 0:HIDDEN], op0=ALU.mult, op1=ALU.subtract).then_inc(w1_low, 1)
                v.wait_ge(bias_loaded, 16 * 6)
                link(nc.vector.tensor_scalar(bf[:], bf[:], WSCALE, None, ALU.mult))
                link(nc.vector.tensor_copy(bhi[:], bf[:]))
                link(nc.vector.scalar_tensor_tensor(out=bres[:], in0=bhi[:], scalar=cf[:, C_PART:C_PART + 1], in1=bf[:],
                                                    op0=ALU.mult, op1=ALU.add))
                link(nc.vector.tensor_copy(bhi[:], bres[:]))
                nc.vector.scalar_tensor_tensor(out=bias[:], in0=bhi[:], scalar=cf[:, C_PART + 1:C_PART + 2], in1=bres[:],
                                               op0=ALU.mult, op1=ALU.add).then_inc(bias_ready, 1)

            def act_split(f, i, s):
                n, r = f * NT + i * TURN + s, s % RING
                v.wait_ge(gelu_ready, n + 1)
                if later(f, i) or s >= RING:
                    v.wait_ge(y_ready, n + (1 - RING))
                nc.vector.tensor_copy(acth[:, r, :], act[:, r, :]).then_inc(acth_ready, 1)
                v.wait_ge(acth_ready, n + 1)
                nc.vector.tensor_tensor(actl[:, r, :], act[:, r, :], acth[:, r, :], ALU.subtract).then_inc(actl_ready, 1)

            def experts(f):
                for s in range(TURN):
                    act_split(f, 0, s)
                with v.Fori(1, TURNS) as i:
                    for s in range(TURN):
                        act_split(f, i, s)

            def add_ffn(f, g):
                for t in range(GT):
                    v.wait_ge(back_done[g][t], 16 * (f + 1))
                    last = nc.vector.scalar_tensor_tensor(out=x[:, g * GT + t, :], in0=yback[g][:, t, :], scalar=coef[g][:, t:t + 1],
                                                          in1=x[:, g * GT + t, :], op0=ALU.mult, op1=ALU.add)
                    if f == 1:
                        last.then_inc(x_final, 1)
                if f == 0:
                    link(last)

            def attend(g, h):
                a = 2 * g + h
                seq3 = [P, 2, SEQ]

                def table(c):
                    return cf[:, None, c:c + SEQ].to_broadcast(seq3)

                def two(ap):
                    return ap.rearrange("p (b s) -> p b s", b=2)

                v.wait_ge(q_ready, a + 1)
                if a:
                    v.wait_ge(att_ready, 2 * a)
                nc.vector.tensor_tensor(two(t1[:]), two(bank[0][:]), table(C_COST), ALU.mult)
                link(nc.vector.tensor_tensor(two(t2[:]), two(bank[1][:]), table(C_SINT), ALU.mult))
                nc.vector.tensor_tensor(qr[:], t1[:], t2[:], ALU.add).then_inc(qr_ready, 1)
                v.wait_ge(k_ready, a + 1)
                nc.vector.tensor_tensor(two(t3[:]), two(bank[4][:]), table(C_COSR), ALU.mult)
                link(nc.vector.tensor_tensor(two(t4[:]), two(bank[5][:]), table(C_SINR), ALU.mult))
                nc.vector.tensor_tensor(kr[:], t3[:], t4[:], ALU.add).then_inc(kr_ready, 1)
                v.wait_ge(vpad_ready, a + 1)
                link(nc.vector.tensor_scalar(local[:], vpad[:, :, 0:SEQ], lepe[:, 0:1], lepe[:, TAPS:TAPS + 1], ALU.mult, ALU.add))
                for k in range(1, TAPS):
                    link(nc.vector.scalar_tensor_tensor(out=local[:], in0=vpad[:, :, k:k + SEQ], scalar=lepe[:, k:k + 1],
                                                        in1=local[:], op0=ALU.mult, op1=ALU.add))
                v.wait_ge(kv_ready, a + 1)
                for b in range(2):
                    kv = bank[7][:, b * (P + 1):(b + 1) * (P + 1)]
                    nc.vector.tensor_tensor(kvm[:, b, :], kv[:, 0:P], mask, ALU.mult)
                    last = nc.vector.tensor_scalar(ksm[:, b, :], mask, kv[:, P:P + 1], None, ALU.mult)
                last.then_inc(kvm_ready, 1)
                for b in range(2):
                    v.wait_ge(den_copied, 2 * a + b + 1)
                    link(nc.vector.reciprocal(rden[:, b, :], den[:, b, :]))
                    nc.vector.scalar_tensor_tensor(out=att[:, b, :], in0=bank[4 + b][:, 0:SEQ], scalar=vsum[:, b:b + 1],
                                                   in1=rden[:, b, :], op0=ALU.add, op1=ALU.mult).then_inc(att_ready, 1)
                v.wait_ge(att_ready, 2 * a + 2)
                link(nc.vector.tensor_tensor(att[:], att[:], local[:], ALU.add))
                v.wait_ge(gate_copied, a + 1)
                nc.vector.tensor_tensor(two(gated[:]), att[:], two(gate[:]), ALU.mult).then_inc(gated_ready, 1)
                v.wait_ge(proj_ready, a + 1)
                rows = x[:, g * GT + 4 * h:g * GT + 4 * h + 4, :]
                nc.vector.tensor_tensor(rows, bank[6][:].rearrange("p (t c) -> p t c", t=4), rows, ALU.add).then_inc(x_updated, 1)

            v.wait_ge(consts_loaded, 16 * 4)
            v.wait_ge(pool_set, 1)
            for g in range(GROUPS):
                v.wait_ge(x_in_sem[g], 16)
                norm(NORM[0, g], g)
                split(NORM[0, g], 0, g)
                route(0, g)
            tables()
            experts(0)
            v.wait_ge(attn_loaded, 32)
            for g in range(GROUPS):
                add_ffn(0, g)
                norm(NORM["a", g], g)
                for h in range(2):
                    attend(g, h)
                v.wait_ge(x_updated, 2 * g + 2)
                norm(NORM[1, g], g)
                split(NORM[1, g], 1, g)
                route(1, g)
            experts(1)
            for g in range(GROUPS):
                add_ffn(1, g)

        @block.tensor
        def _(pe):
            def norm(k, g):
                for h in range(2):
                    pe.wait_ge(xn_ready, 2 * k + h + 1)
                    if k:
                        pe.wait_ge(xnT_ready, 2 * k)
                    for t in range(4):
                        last = nc.tensor.transpose(bank[6 + h][:, t * P:(t + 1) * P], xn[:, 4 * h + t, :], ident)
                    last.then_inc(xn_turned, 1)

            def route(k, f, g):
                n = GROUPS * f + g
                if n:
                    pe.wait_ge(pos_ready, n)
                for t in range(GT):
                    pe.wait_ge(xnT_ready, 2 * k + t // 4 + 1)
                    last = nc.tensor.matmul(bank[5][:, t * EXPERTS:(t + 1) * EXPERTS], xnT[g][:, t * P:(t + 1) * P], wr[:],
                                            start=True, stop=True)
                last.then_inc(logits_ready, 1)
                pe.wait_ge(onehot_ready, n + 1)
                hot = onehot[:].rearrange("p t e -> p (t e)")
                nc.tensor.matmul(bank[4][:, 0:GE], before, hot, start=True, stop=False, skip_group_check=True)
                for d in range(1, GT):
                    nc.tensor.matmul(bank[4][:, d * EXPERTS:GE], ones16, hot[:, 0:GE - d * EXPERTS], start=False, stop=False,
                                     skip_group_check=True)
                for t in range(GT):
                    last = nc.tensor.matmul(bank[4][:, GE:GE + EXPERTS], ones16, onehot[:, t, :], start=False,
                                            stop=(t == GT - 1), skip_group_check=True)
                last.then_inc(ranks_ready, 1)

            def turn(f, i, s):
                n = f * NT + i * TURN + s
                if s % RING == 0:
                    pe.wait_ge(x_landed[s // RING], f * (16 * TURNS) + i * 16 + 16)
                if later(f, i) or s > 0:
                    pe.wait_ge(tileT_ready, n)
                xt = bank[6 + s % 2][:, 0:P].bitcast(F16)
                for k in range(2):
                    last = nc.tensor.transpose(xt[:, k * P:(k + 1) * P], ringX[:, s, k * D:(k + 1) * D], ident16)
                last.then_inc(tile_turned, 1)

            def hidden(f, i, s):
                n = f * NT + i * TURN + s
                pe.wait_ge(w_landed[s], f * (16 * TURNS) + i * 16 + 16)
                pe.wait_ge(tileT_ready, n + 1)
                if later(f, i) or s >= RING:
                    pe.wait_ge(gelu_ready, n + (1 - RING))
                hb, w, r = bank[s % RING], ringW[:, s, :], s % RING
                xh, xl = ringT[:, r, 0:P], ringT[:, r, P:2 * P]
                for c in range(HC):
                    nc.tensor.matmul(hb[:, c * P:(c + 1) * P], bias[:, c, :], rowsel[:, bass.ds(i * TURN + s, 1), :],
                                     start=(c == 0), stop=False, skip_group_check=True)
                for c in range(HC):
                    o = hb[:, c * P:(c + 1) * P]
                    hi, lo = w[:, c * P:(c + 1) * P], w[:, HIDDEN + c * P:HIDDEN + (c + 1) * P]
                    nc.tensor.matmul(o, hi, xh, start=False, stop=False, skip_group_check=True)
                    nc.tensor.matmul(o, hi, xl, start=False, stop=False, skip_group_check=True)
                    last = nc.tensor.matmul(o, lo, xh, start=False, stop=(c == HC - 1), skip_group_check=True)
                last.then_inc(hid_ready, 1)

            def project(f, i, s):
                n, r = f * NT + i * TURN + s, s % RING
                pe.wait_ge(actl_ready, n + 1)
                if later(f, i) or s >= RING:
                    pe.wait_ge(y_copied, n + (1 - RING))
                o, w = bank[3 + r][:, 0:D], ringW[:, s, 2 * HIDDEN:]
                nc.tensor.matmul(o, rowsel[:, bass.ds(i * TURN + s, 1), :], bias[:, HC, :], start=True, stop=False)
                for c in range(HC):
                    hi, lo = w[:, c * P:(c + 1) * P], w[:, HIDDEN + c * P:HIDDEN + (c + 1) * P]
                    ah, al = acth[:, r, c * P:(c + 1) * P], actl[:, r, c * P:(c + 1) * P]
                    nc.tensor.matmul(o, ah, hi, start=False, stop=False)
                    nc.tensor.matmul(o, ah, lo, start=False, stop=False)
                    last = nc.tensor.matmul(o, al, hi, start=False, stop=(c == HC - 1))
                last.then_inc(y_ready, 1)

            def step(f, i, s, last=False):
                if not last or s + 3 < TURN:
                    turn(f, *ahead(i, s, 3))
                if not last or s + 2 < TURN:
                    hidden(f, *ahead(i, s, 2))
                project(f, i, s)

            def experts(f):
                for s in range(3):
                    turn(f, 0, s)
                if f == 0:
                    pe.wait_ge(bias_ready, 1)
                pe.wait_ge(rowsel_ready, GROUPS * f + 1)
                for s in range(2):
                    hidden(f, 0, s)
                pe.wait_ge(pos_ready, GROUPS * (f + 1))
                for s in range(TURN):
                    step(f, 0, s)
                pe.wait_ge(rowsel_ready, GROUPS * f + 2)
                with pe.Fori(1, TURNS - 1) as i:
                    for s in range(TURN):
                        step(f, i, s)
                for s in range(TURN):
                    step(f, TURNS - 1, s, last=True)

            def attend(g, h):
                a = 2 * g + h
                xt = xnT[g][:, h * HALF:(h + 1) * HALF]
                if a:
                    pe.wait_ge(qr_ready, a)
                    pe.wait_ge(vpad_ready, a)
                    pe.wait_ge(gate_copied, a)
                    pe.wait_ge(att_ready, 2 * a)
                    pe.wait_ge(x_updated, a)
                nc.tensor.matmul(bank[0][:], wattn[:, 0, :], xt, start=True, stop=True)
                nc.tensor.matmul(bank[1][:], wattn[:, 1, :], xt, start=True, stop=True).then_inc(q_ready, 1)
                nc.tensor.matmul(bank[2][:], wattn[:, 2, :], xt, start=True, stop=True).then_inc(v_ready, 1)
                nc.tensor.matmul(bank[3][:], wattn[:, 3, :], xt, start=True, stop=True).then_inc(gate_ready, 1)
                for w, b, done in ((4, 4, None), (5, 5, k_ready), (2, 6, vrow_ready)):
                    for t in range(4):
                        last = nc.tensor.matmul(bank[b][:, t * P:(t + 1) * P], xt[:, t * P:(t + 1) * P], wattn[:, w, :],
                                                start=True, stop=True)
                    if done:
                        last.then_inc(done, 1)
                pe.wait_ge(kr_ready, a + 1)
                pe.wait_ge(vrow_copied, a + 1)
                for b in range(2):
                    for t in range(2):
                        last = nc.tensor.matmul(bank[7][:, b * (P + 1):(b + 1) * (P + 1)], kr[:, (2 * b + t) * P:(2 * b + t + 1) * P],
                                                vrow[:, 2 * b + t, :], start=(t == 0), stop=(t == 1))
                last.then_inc(kv_ready, 1)
                pe.wait_ge(kvm_ready, a + 1)
                pe.wait_ge(qr_ready, a + 1)
                for b in range(2):
                    q = qr[:, b * SEQ:(b + 1) * SEQ]
                    nc.tensor.matmul(bank[4 + b][:, 0:SEQ], kvm[:, b, :], q, start=True, stop=True)
                    nc.tensor.matmul(bank[4 + b][:, SEQ:2 * SEQ], ksm[:, b, :], q, start=True, stop=True).then_inc(nd_ready, 1)
                pe.wait_ge(gated_ready, a + 1)
                for t in range(4):
                    last = nc.tensor.matmul(bank[6][:, t * P:(t + 1) * P], gated[:, t * P:(t + 1) * P], wattn[:, 6, :],
                                            start=True, stop=True)
                last.then_inc(proj_ready, 1)

            pe.wait_ge(consts_loaded, 16 * 4)
            for g in range(GROUPS):
                norm(NORM[0, g], g)
                route(NORM[0, g], 0, g)
            experts(0)
            pe.wait_ge(attn_loaded, 32)
            pe.wait_ge(y_copied, NT)
            for g in range(GROUPS):
                norm(NORM["a", g], g)
                pe.wait_ge(xnT_ready, 2 * NORM["a", g] + 2)
                if g:
                    pe.wait_ge(pos_ready, GROUPS + g)
                for h in range(2):
                    attend(g, h)
                norm(NORM[1, g], g)
                route(NORM[1, g], 1, g)
            experts(1)


def kernel(**inputs):
    import concourse.bacc as bacc
    from concourse.bass_utils import run_bass_kernel_spmd

    def arr(name):
        return np.ascontiguousarray(inputs[name])

    def turned(name):
        return np.asarray(inputs[name]).T

    swap = (np.arange(P) // DK) * DK + (np.arange(P) + DK // 2) % DK
    q, k = turned("L0_attn_Wq"), turned("L0_attn_Wk")
    wattn = np.stack([q, q[:, swap], turned("L0_attn_Wv"), turned("L0_attn_Wg"), k, k[:, swap], turned("L0_attn_Wo")], axis=1)
    lepe = np.concatenate([arr("L0_attn_lepe_w").reshape(D, TAPS), arr("L0_attn_lepe_b").reshape(D, 1)], axis=1)
    cf, ch = constants()
    arrays = {
        "x_in": arr("L0_attn_hidden_states").reshape(TOKENS, D),
        "wr_in": arr("L0_ffn_Wr"), "br_in": arr("L0_ffn_br").reshape(1, EXPERTS),
        "w1_in": arr("L0_ffn_W1"), "b1_in": arr("L0_ffn_b1"), "w2_in": arr("L0_ffn_W2"), "b2_in": arr("L0_ffn_b2"),
        "wattn_in": np.ascontiguousarray(wattn), "lepe_in": np.ascontiguousarray(lepe), "cf_in": cf, "ch_in": ch,
    }
    nc = bacc.Bacc("TRN2", target_bir_lowering=False, num_devices=1)
    args = [nc.dram_tensor(n, a.shape, mybir.dt.from_np(a.dtype), kind="ExternalInput").ap() for n, a in arrays.items()]
    out = nc.dram_tensor("out", [TOKENS, D], F32, kind="ExternalOutput").ap()
    program(nc, *args, out)
    r = run_bass_kernel_spmd(nc, [arrays], core_ids=[0])
    return r.results[0]["out"].reshape(TOKENS // SEQ, SEQ, D)
```

```python
from contextlib import ExitStack

import numpy as np

import concourse.bass as bass
from concourse import mybir

P = 128
D = 128
TOKENS, SEQ = 2048, 256
HEADS, DK = 8, 16
EXPERTS, HIDDEN = 8, 512
HC = HIDDEN // P
GROUPS = 2
GT = TOKENS // GROUPS // P
GE = GT * EXPERTS
GTILES = (TOKENS // GROUPS - EXPERTS) // P + EXPERTS
NT = GROUPS * GTILES
SLOTS = NT * P
RING = 3
TURN = 6
TURNS = NT // TURN
COPIED = (2, 5)
HALF = 512
TAPS = 5
EPS = 1e-5
WSCALE = 64.0
WCOLS = 4 * HIDDEN
ROW = WCOLS // 2 + HC

F32, F16, BF16 = mybir.dt.float32, mybir.dt.float16, mybir.dt.bfloat16
I32, U32 = mybir.dt.int32, mybir.dt.uint32
ALU = mybir.AluOpType
ACT = mybir.ActivationFunctionType
X = mybir.AxisListType.X

C_ID, C_MASK, C_RANK = 0, P, 2 * P
C_TILE = C_RANK + EXPERTS
C_PART = C_TILE + GTILES
C_COST = C_PART + 3
C_SINT, C_COSR, C_SINR, C_END = C_COST + SEQ, C_COST + 2 * SEQ, C_COST + 3 * SEQ, C_COST + 4 * SEQ


def constants():
    f = np.zeros((P, C_END), np.float32)
    f[:, C_ID:C_ID + P] = np.eye(P)
    head = np.arange(P) // DK
    f[:, C_MASK:C_MASK + P] = (head[:, None] == head[None, :]) * np.float32(DK ** -0.5)
    inv = (1.0 / np.float32(10000.0) ** (np.arange(0, DK, 2, dtype=np.float32) / np.float32(DK))).astype(np.float32)
    ang = np.arange(SEQ, dtype=np.float32)[:, None] * inv[None, :]
    ang = np.tile(np.concatenate([ang, ang], axis=1), (1, HEADS))
    sign = np.where(np.arange(P) % DK < DK // 2, -1.0, 1.0).astype(np.float32)
    cos, sin = np.cos(ang).astype(np.float32), np.sin(ang).astype(np.float32) * sign[None, :]
    f[:, C_COST:C_COST + SEQ], f[:, C_SINT:C_SINT + SEQ] = cos.T, sin.T
    f[:, C_COSR:C_COSR + SEQ] = cos.reshape(2, P, P).transpose(1, 0, 2).reshape(P, SEQ)
    f[:, C_SINR:C_SINR + SEQ] = sin.reshape(2, P, P).transpose(1, 0, 2).reshape(P, SEQ)
    f[:, C_RANK:C_RANK + EXPERTS] = EXPERTS - np.arange(EXPERTS)
    f[:, C_TILE:C_TILE + GTILES] = np.arange(GTILES)
    part, expert = np.arange(P) // EXPERTS, np.arange(P) % EXPERTS
    f[:, C_PART] = -(part >= 1).astype(np.float32)
    f[:, C_PART + 1] = -(part >= 2).astype(np.float32)
    f[:, C_PART + 2] = np.where(part < 3, expert, -1)
    h = np.zeros((P, 3 * P), np.float16)
    h[:, 0:P] = np.eye(P)
    h[:, P:2 * P] = np.triu(np.ones((P, P)), 1)
    h[:, 2 * P:3 * P] = 1
    return f, h


def program(nc, x_in, wr_in, br_in, w1_in, b1_in, w2_in, b2_in, wattn_in, lepe_in, cf_in, ch_in, out):
    with ExitStack() as ctx:
        def sb(name, shape, dt=F32):
            return ctx.enter_context(nc.sbuf_tensor(name, shape, dt))

        def sem(name):
            return ctx.enter_context(nc.semaphore(name))

        sorted_x = nc.dram_tensor("sorted_x", [SLOTS, 2 * D], F16, kind="Internal").ap()
        sorted_y = nc.dram_tensor("sorted_y", [SLOTS, D], F32, kind="Internal").ap()

        bank = [ctx.enter_context(nc.psum_tensor(f"bank{i}", [P, 512], F32)) for i in range(8)]

        cf, ch = sb("cf", [P, C_END]), sb("ch", [P, 3 * P], F16)
        ident, mask = cf[:, C_ID:C_ID + P], cf[:, C_MASK:C_MASK + P]
        rank = cf[:, C_RANK:C_RANK + EXPERTS]
        ident16, before, ones16 = ch[:, 0:P], ch[:, P:2 * P], ch[:, 2 * P:3 * P]
        x = sb("x", [P, GROUPS * GT, D])
        wr, br = sb("wr", [P, EXPERTS]), sb("br", [P, EXPERTS])
        wattn = sb("wattn", [P, 6, P])
        lepe = sb("lepe", [P, TAPS + 1])
        w1f, w2f = sb("w1f", [P, EXPERTS, HIDDEN]), sb("w2f", [P, EXPERTS, HIDDEN])
        b1 = sb("b1", [P, EXPERTS, HC])
        bf, bres = sb("bf", [P, D]), sb("bres", [P, D])
        bhi, bias = sb("bhi", [P, D], BF16), sb("bias", [P, D], BF16)
        rows32 = sb("rows32", [P, EXPERTS, ROW])
        table = rows32[:, :, 0:WCOLS // 2].bitcast(F16)
        zeros = sb("zeros", [P, 2 * D], F16)

        bn, mv = sb("bn", [P, GT, 6]), sb("mv", [P, GT, 2])
        std, rstd, shift, eps = sb("std", [P, GT]), sb("rstd", [P, GT]), sb("shift", [P, GT]), sb("eps", [P, 1])
        xn = [sb(f"xn{g}", [P, GT, D]) for g in range(GROUPS)]
        xs = [sb(f"xs{g}", [P, GT, 2 * D], F16) for g in range(GROUPS)]
        xnT = [sb(f"xnT{g}", [P, GT * P]) for g in range(GROUPS)]
        lg, top = sb("lg", [P, GT, EXPERTS]), sb("top", [P, GT])
        ld = [sb(f"ld{g}", [P, GT, EXPERTS]) for g in range(GROUPS)]
        score, best = sb("score", [P, GT, EXPERTS]), sb("best", [P, GT])
        onehot = sb("onehot", [P, GT, EXPERTS], F16)
        ex, exsum = [sb(f"ex{g}", [P, GT, EXPERTS]) for g in range(GROUPS)], sb("exsum", [P, GT])
        coef = [sb(f"coef{g}", [P, GT]) for g in range(GROUPS)]
        cnt, tiles = sb("cnt", [P, EXPERTS], I32), sb("tiles", [P, EXPERTS], I32)
        cum, first = sb("cum", [P, EXPERTS]), sb("first", [P, EXPERTS])
        posw, posf = sb("posw", [P, GT, EXPERTS]), sb("posf", [P, GT])
        pos = [sb(f"pos{g}", [P, GT], U32) for g in range(GROUPS)]
        over, owner = sb("over", [P, GTILES, EXPERTS]), sb("owner", [P, GTILES])
        expert = sb("expert", [P, NT], I32)
        isrow = sb("isrow", [P, NT], F16)
        ones1 = sb("ones1", [P, EXPERTS])

        ring32 = sb("ring32", [P, TURN, ROW])
        ringW = ring32[:, :, 0:WCOLS // 2].bitcast(F16)
        ringX, ringT = sb("ringX", [P, TURN, 2 * D], F16), sb("ringT", [P, RING, 2 * P], F16)
        act = sb("act", [P, RING, HIDDEN])
        acth, actl = sb("acth", [P, RING, HIDDEN], F16), sb("actl", [P, RING, HIDDEN], F16)
        ybuf = sb("ybuf", [P, TURN, D])
        yback = [sb(f"yback{g}", [P, GT, D]) for g in range(GROUPS)]

        t1, t2, t3, t4 = (sb(f"t{i}", [P, HALF]) for i in range(4))
        qr, kr = sb("qr", [P, 2, HALF]), sb("kr", [P, HALF])
        vpad, vsum = sb("vpad", [P, 2, 2, SEQ + TAPS - 1]), sb("vsum", [P, 2, 2])
        gate = sb("gate", [P, 2, HALF])
        vrow = sb("vrow", [P, 4, P + 1])
        kvm, ksm = sb("kvm", [P, 2, P]), sb("ksm", [P, 2, HEADS])
        den, rden = sb("den", [P, 4, HEADS]), sb("rden", [P, 4, HEADS])
        rspread, num = sb("rspread", [P, 4 * HEADS, DK]), sb("num", [P, 2, SEQ])
        local, att = sb("local", [P, 2, 2, SEQ]), sb("att", [P, 2, SEQ])

        x_in_sem = [sem(f"x_loaded{g}") for g in range(GROUPS)]
        consts_loaded, attn_loaded = sem("consts_loaded"), sem("attn_loaded")
        w1_loaded = [sem(f"w1_loaded{h}") for h in range(2)]
        w2_loaded = [sem(f"w2_loaded{h}") for h in range(4)]
        bias_zeroed, bias_loaded, b1_loaded = sem("bias_zeroed"), sem("bias_loaded"), sem("b1_loaded")
        zeros_set, pool_set = sem("zeros_set"), sem("pool_set")
        slots_cleared = [sem(f"slots_cleared{g}") for g in range(GROUPS)]
        w1_high, w2_high, bias_step, bias_ready = (
            sem(n) for n in ("w1_high", "w2_high", "bias_step", "bias_ready"))
        w1_scaled = sem("w1_scaled")
        low_pool, low_dve = sem("low_pool"), sem("low_dve")
        stats_ready, std_ready, scale_ready = sem("stats_ready"), sem("std_ready"), sem("scale_ready")
        xn_ready = [sem(f"xn_ready{h}") for h in range(2)]
        xn_turned, xnT_ready = sem("xn_turned"), sem("xnT_ready")
        logits_ready, shifted_ready, exp_ready = sem("logits_ready"), sem("shifted_ready"), sem("exp_ready")
        onehot_ready, ranks_ready = sem("onehot_ready"), sem("ranks_ready")
        pos_ready, expert_ready, xs_ready = sem("pos_ready"), sem("expert_ready"), sem("xs_ready")
        isrow_ready = sem("isrow_ready")
        sorted_done = [sem(f"sorted_done{g}") for g in range(GROUPS)]
        back_done = [[sem(f"back_done{g}_{t}") for t in range(GT)] for g in range(GROUPS)]
        w_landed = [sem(f"w_landed{s}") for s in range(TURN)]
        w_copied = sem("w_copied")
        x_landed = [sem(f"x_landed{q}") for q in range(2)]
        y_stored = [sem(f"y_stored{q}") for q in range(2)]
        tile_turned, tileT_ready = sem("tile_turned"), sem("tileT_ready")
        hid_ready, gelu_ready = sem("hid_ready"), sem("gelu_ready")
        acth_ready, actl_ready = sem("acth_ready"), sem("actl_ready")
        y_ready, y_copied = sem("y_ready"), sem("y_copied")
        q_ready, v_ready, gate_ready, k_ready, vrow_ready = (
            sem(n) for n in ("q_ready", "v_ready", "gate_ready", "k_ready", "vrow_ready"))
        q_used, k_used, conv_done = sem("q_used"), sem("k_used"), sem("conv_done")
        qr_ready, kr_ready, vpad_ready, gate_copied, vrow_copied = (
            sem(n) for n in ("qr_ready", "kr_ready", "vpad_ready", "gate_copied", "vrow_copied"))
        kv_ready, kvm_ready, den_ready, rden_ready, rspread_ready, num_ready, att_ready = (
            sem(n) for n in ("kv_ready", "kvm_ready", "den_ready", "rden_ready", "rspread_ready", "num_ready", "att_ready"))
        num_copied, rdenT_ready = sem("num_copied"), sem("rdenT_ready")
        tap_ready = sem("tap_ready")
        gated_ready, proj_ready, x_updated = sem("gated_ready"), sem("proj_ready"), sem("x_updated")
        x_final, stored = sem("x_final"), sem("stored")
        dve_step = sem("dve_step")

        HE = [slice(h * EXPERTS // 2, (h + 1) * EXPERTS // 2) for h in range(2)]
        QE = [slice(h * EXPERTS // 4, (h + 1) * EXPERTS // 4) for h in range(4)]
        NORM = {(0, 0): 0, (0, 1): 1, ("a", 0): 2, ("a", 1): 3, (1, 0): 4, (1, 1): 5}

        BEFORE = {2: 0, 3: 1, 4: 2, 5: 3}
        ROUTED = {1: 1, 2: 2, 3: 2, 4: 2, 5: 3}

        def norm_bank(k, h):
            return 6 + h if k == 0 else 5 + h if k == 2 else 5

        def ahead(i, s, d):
            return i + (s + d) // TURN, (s + d) % TURN

        def later(f, i):
            return f > 0 or not isinstance(i, int) or i > 0

        block = ctx.enter_context(nc.Block())

        @block.sync
        def _(sp):
            def load_rows(g):
                sp.dma_start(x[:, g * GT:(g + 1) * GT, :],
                             x_in[g * GT * P:(g + 1) * GT * P, :].rearrange("(t p) d -> p t d", p=P)
                             ).then_inc(x_in_sem[g], 16)

            def clear_slots(g):
                own = slice(g * GTILES * P, (g + 1) * GTILES * P)
                sp.dma_start(sorted_x[own, :].rearrange("(n p) d -> p n d", p=P),
                             zeros[:, None, :].to_broadcast([P, GTILES, 2 * D])).then_inc(slots_cleared[g], 16)

            load_rows(0)
            sp.dma_start(cf[:, 0:C_COST], cf_in[:, 0:C_COST]).then_inc(consts_loaded, 16)
            sp.dma_start(ch[:], ch_in).then_inc(consts_loaded, 16)
            sp.dma_start(wr[:], wr_in).then_inc(consts_loaded, 16)
            sp.dma_start(br[:], br_in.to_broadcast([P, EXPERTS])).then_inc(consts_loaded, 16)
            load_rows(1)
            for h in range(2):
                sp.dma_start(w1f[:, HE[h], :], w1_in[HE[h]].rearrange("e d h -> d e h")).then_inc(w1_loaded[h], 16)
            sp.wait_ge(zeros_set, 1)
            clear_slots(0)
            for h in range(4):
                sp.dma_start(w2f[:, QE[h], :].rearrange("p e (c d) -> p e c d", c=HC),
                             w2_in[QE[h]].rearrange("e (c p) d -> p e c d", p=P)).then_inc(w2_loaded[h], 16)
            clear_slots(1)
            sp.dma_start(cf[:, C_COST:], cf_in[:, C_COST:]).then_inc(attn_loaded, 16)
            sp.dma_start(wattn[:], wattn_in).then_inc(attn_loaded, 16)
            sp.dma_start(lepe[:], lepe_in).then_inc(attn_loaded, 16)

            def load_tile_rows(f, i, q):
                if later(f, i):
                    sp.wait_ge(tile_turned, f * NT + i * TURN + (q * RING + RING - TURN))
                row = i * (TURN * P) + q * RING * P
                sp.dma_start(ringX[:, q * RING:(q + 1) * RING, :],
                             sorted_x[bass.ds(row, RING * P), :].rearrange("(t p) d -> p t d", p=P)).then_inc(x_landed[q], 16)

            def load_weights(f, i, s):
                if s in COPIED:
                    return
                tile = i * TURN + s
                e = sp.value_load(expert[0:1, bass.ds(tile, 1)], min_val=0, max_val=EXPERTS - 1)
                if later(f, i):
                    sp.wait_ge(y_ready, f * NT + i * TURN + (s + 1 - TURN))
                sp.dma_start(ring32[:, s, :], rows32[:, bass.ds(e, 1), :]).then_inc(w_landed[s], 16)

            def turn(f, i):
                for s in range(TURN):
                    if s % RING == 0:
                        load_tile_rows(f, i, s // RING)
                    load_weights(f, i, s)

            def first_turn(f):
                sp.wait_ge(expert_ready, GROUPS * f + 1)
                for s in range(RING):
                    load_weights(f, 0, s)
                sp.wait_ge(sorted_done[0], 16 * GT * (f + 1))
                for q in range(2):
                    load_tile_rows(f, 0, q)
                for s in range(RING, TURN):
                    load_weights(f, 0, s)

            def middle_turn(f, i):
                load_tile_rows(f, i, 0)
                for s in range(RING):
                    load_weights(f, i, s)
                sp.wait_ge(expert_ready, GROUPS * f + 2)
                sp.wait_ge(sorted_done[1], 16 * GT * (f + 1))
                load_tile_rows(f, i, 1)
                for s in range(RING, TURN):
                    load_weights(f, i, s)

            sp.wait_ge(low_pool, 1)
            sp.wait_ge(low_dve, 6)
            for f in range(2):
                first_turn(f)
                turn(f, 1)
                middle_turn(f, GTILES // TURN)
                with sp.Fori(GTILES // TURN + 1, TURNS) as i:
                    turn(f, i)
            for g in range(GROUPS):
                for t in range(0, GT, 2):
                    n = g * GT + t
                    sp.wait_ge(x_final, n + 2)
                    sp.dma_start(out[n * P:(n + 2) * P, :].rearrange("(t p) d -> p t d", p=P),
                                 x[:, n:n + 2, :]).then_inc(stored, 16)
            sp.wait_ge(stored, 16 * GROUPS * GT // 2)

        @block.gpsimd
        def _(pool):
            nc.gpsimd.memset(bf[:], 0.0).then_inc(bias_zeroed, 1)
            nc.gpsimd.memset(zeros[:], 0.0).then_inc(zeros_set, 1)
            nc.gpsimd.memset(vpad[:], 0.0)
            nc.gpsimd.memset(ones1[:], 1.0)
            nc.gpsimd.memset(eps[:], EPS)
            nc.gpsimd.memset(vrow[:], 1.0).then_inc(pool_set, 1)

            def sort_out(f, g):
                pool.wait_ge(xs_ready, GROUPS * f + g + 1)
                pool.wait_ge(pos_ready, GROUPS * f + g + 1)
                pool.wait_ge(slots_cleared[g], 16)
                for t in range(GT):
                    nc.gpsimd.indirect_dma_start(
                        out=sorted_x, out_offset=bass.IndirectOffsetOnAxis(ap=pos[g][:, t:t + 1], axis=0),
                        in_=xs[g][:, t, :], in_offset=None).then_inc(sorted_done[g], 16)

            def sort_back(f, g):
                tiles_before = f * NT + (g + 1) * GTILES
                for q in range(2):
                    pool.wait_ge(y_stored[q], 16 * ((tiles_before // RING + 1 - q) // 2))
                for t in range(GT):
                    nc.gpsimd.indirect_dma_start(
                        out=yback[g][:, t, :], out_offset=None, in_=sorted_y[0:(g + 1) * GTILES * P, :],
                        in_offset=bass.IndirectOffsetOnAxis(ap=pos[g][:, t:t + 1], axis=0)).then_inc(back_done[g][t], 16)

            def rotate(a):
                pool.wait_ge(k_used, a + 1)
                nc.gpsimd.tensor_tensor(kr[:], t3[:], t4[:], ALU.add).then_inc(kr_ready, 1)
                pool.wait_ge(q_used, a + 1)
                nc.gpsimd.tensor_tensor(qr[:, a % 2, :], t1[:], t2[:], ALU.add).then_inc(qr_ready, 1)

            pool.wait_ge(w1_high, 1)
            nc.gpsimd.tensor_tensor(table[:, HE[0], HIDDEN:2 * HIDDEN], w1f[:, HE[0], :], table[:, HE[0], 0:HIDDEN],
                                    ALU.subtract).then_inc(low_pool, 1)
            sort_out(0, 0)
            sort_out(0, 1)
            sort_back(0, 0)
            sort_back(0, 1)
            rotate(2)
            rotate(3)
            sort_out(1, 0)
            sort_out(1, 1)
            sort_back(1, 0)
            sort_back(1, 1)

        @block.scalar
        def _(sc):
            def deviations(k):
                sc.wait_ge(stats_ready, k + 1)
                nc.scalar.activation(std[:], mv[:, :, 1], ACT.Sqrt, bias=eps[:]).then_inc(std_ready, 1)

            def normalize(k, g):
                sc.wait_ge(scale_ready, k + 1)
                if k in BEFORE:
                    sc.wait_ge(xn_turned, 2 * BEFORE[k] + 2)
                    sc.wait_ge(xs_ready, ROUTED[k])
                for t in range(GT // 2, GT):
                    last = nc.scalar.activation(xn[g][:, t, :], x[:, g * GT + t, :], ACT.Identity, scale=rstd[:, t:t + 1],
                                                bias=shift[:, t:t + 1])
                last.then_inc(xn_ready[1], 1)

            def norm(k, g, h):
                sc.wait_ge(xn_turned, 2 * k + h + 1)
                nc.scalar.copy(xnT[g][:, h * HALF:(h + 1) * HALF], bank[norm_bank(k, h)][:]).then_inc(xnT_ready, 1)

            def probability(f, g):
                sc.wait_ge(shifted_ready, GROUPS * f + g + 1)
                nc.scalar.activation(ex[g][:], ld[g][:], ACT.Exp).then_inc(exp_ready, 1)

            def turn_copy(f, i, s):
                n = f * NT + i * TURN + s
                sc.wait_ge(tile_turned, n + 1)
                if later(f, i) or s >= RING:
                    sc.wait_ge(hid_ready, n + (1 - RING))
                nc.scalar.copy(ringT[:, s % RING, :], bank[6 + s % 2][:, 0:P].bitcast(F16)).then_inc(tileT_ready, 1)

            def gelu(f, i, s):
                n = f * NT + i * TURN + s
                sc.wait_ge(hid_ready, n + 1)
                if later(f, i) or s >= RING:
                    sc.wait_ge(actl_ready, n + (1 - RING))
                b = ring32[:, s, WCOLS // 2:]
                for c in range(HC):
                    own = slice(c * P, (c + 1) * P)
                    last = nc.scalar.activation(act[:, s % RING, own], bank[s % RING][:, own], ACT.Gelu, scale=1.0 / WSCALE,
                                                bias=b[:, c:c + 1])
                last.then_inc(gelu_ready, 1)

            def y_copy(f, i, s):
                q = s // RING
                sc.wait_ge(y_ready, f * NT + i * TURN + s + 1)
                if s % RING == 0 and later(f, i):
                    sc.wait_ge(y_stored[q], f * (16 * TURNS) + i * 16)
                nc.scalar.activation(ybuf[:, s, :], bank[3 + s % 2][:, 0:D], ACT.Copy, scale=1.0 / WSCALE).then_inc(y_copied, 1)
                if s % RING == RING - 1:
                    sc.wait_ge(y_copied, f * NT + i * TURN + s + 1)
                    row = i * (TURN * P) + q * RING * P
                    sc.dma_start(sorted_y[bass.ds(row, RING * P), :].rearrange("(t p) d -> p t d", p=P),
                                 ybuf[:, q * RING:(q + 1) * RING, :]).then_inc(y_stored[q], 16)

            def step(f, i, s, first=False, last=False):
                if not last or s + 3 < TURN:
                    turn_copy(f, *ahead(i, s, 3))
                if not first or s:
                    y_copy(f, *ahead(i, s, -1))
                if not last or s + 2 < TURN:
                    gelu(f, *ahead(i, s, 2))
                if first and f == 1 and s < 2:
                    norm(NORM[1, 1], 1, s)
                if last and s == 1 and f == 0:
                    deviations(NORM["a", 0])
                if last and s == 2 and f == 0:
                    normalize(NORM["a", 0], 0)
                if last and s in (3, 4) and f == 0:
                    norm(NORM["a", 0], 0, s - 3)

            def experts(f):
                for s in range(3):
                    turn_copy(f, 0, s)
                if f == 1:
                    deviations(NORM[1, 1])
                    normalize(NORM[1, 1], 1)
                for s in range(2):
                    gelu(f, 0, s)
                for s in range(TURN):
                    step(f, 0, s, first=True)
                with sc.Fori(1, TURNS - 1) as i:
                    for s in range(TURN):
                        step(f, i, s)
                for s in range(TURN):
                    step(f, TURNS - 1, s, last=True)
                y_copy(f, TURNS - 1, TURN - 1)

            def values(a):
                sc.wait_ge(vrow_ready, a + 1)
                nc.scalar.copy(vrow[:, :, 0:P], bank[3][:].rearrange("p (t c) -> p t c", t=4)).then_inc(vrow_copied, 1)
                sc.wait_ge(v_ready, a + 1)
                if a > 1:
                    sc.wait_ge(conv_done, a - 1)
                for b in range(2):
                    last = nc.scalar.activation(vpad[:, a % 2, b, 2:2 + SEQ], bank[4][:, b * SEQ:(b + 1) * SEQ], ACT.Copy,
                                                accum_out=vsum[:, a % 2, b:b + 1])
                last.then_inc(vpad_ready, 1)
                sc.wait_ge(gate_ready, a + 1)
                nc.scalar.copy(gate[:, a % 2, :], bank[1][:]).then_inc(gate_copied, 1)

            def first_tap(a):
                sc.wait_ge(vpad_ready, a + 1)
                if a > 1:
                    sc.wait_ge(gated_ready, a - 1)
                nc.scalar.activation(local[:, a % 2, :, :], vpad[:, a % 2, :, 0:SEQ], ACT.Identity, scale=lepe[:, 0:1],
                                     bias=lepe[:, TAPS:TAPS + 1]).then_inc(tap_ready, 1)

            def spread(a):
                sc.wait_ge(rden_ready, a + 1)
                nc.scalar.copy(rspread[:], rden[:].rearrange("p t h -> p (t h)")[:, :, None].to_broadcast([P, 4 * HEADS, DK])
                               ).then_inc(rspread_ready, 1)

            def numerators(a):
                sc.wait_ge(num_ready, 2 * a + 2)
                for b in range(2):
                    last = nc.scalar.activation(num[:, b, :], bank[7][:, b * SEQ:(b + 1) * SEQ], ACT.Identity,
                                                bias=vsum[:, a % 2, b:b + 1])
                last.then_inc(num_copied, 1)

            sc.wait_ge(bias_zeroed, 1)
            sc.dma_start(bf[0:3 * EXPERTS], b2_in).then_inc(bias_loaded, 16)
            sc.dma_start(b1[:], b1_in).then_inc(b1_loaded, 16)
            sc.wait_ge(pool_set, 1)
            sc.wait_ge(bias_loaded, 16)
            nc.scalar.activation(bf[:], bf[:], ACT.Copy, scale=WSCALE).then_inc(bias_step, 1)
            sc.wait_ge(bias_step, 1)
            nc.scalar.copy(bhi[:], bf[:]).then_inc(bias_step, 1)
            deviations(0)
            sc.wait_ge(bias_step, 3)
            nc.scalar.copy(bhi[:], bres[:]).then_inc(bias_step, 1)
            normalize(0, 0)
            sc.wait_ge(w1_loaded[0], 16)
            nc.scalar.activation(w1f[:, HE[0], :], w1f[:, HE[0], :], ACT.Copy, scale=WSCALE).then_inc(w1_scaled, 1)
            for h in range(2):
                norm(0, 0, h)
            deviations(1)
            normalize(1, 1)
            sc.wait_ge(w1_scaled, 1)
            nc.scalar.copy(table[:, HE[0], 0:HIDDEN], w1f[:, HE[0], :]).then_inc(w1_high, 1)
            sc.wait_ge(w1_loaded[1], 16)
            nc.scalar.activation(table[:, HE[1], 0:HIDDEN], w1f[:, HE[1], :], ACT.Copy, scale=WSCALE).then_inc(w1_high, 1)
            for h in range(4):
                sc.wait_ge(w2_loaded[h], 16)
                nc.scalar.activation(table[:, QE[h], 2 * HIDDEN:3 * HIDDEN], w2f[:, QE[h], :], ACT.Copy,
                                     scale=WSCALE).then_inc(w2_high, 1)
                if h % 2:
                    norm(1, 1, h // 2)
            probability(0, 0)
            experts(0)
            values(0)
            first_tap(0)
            probability(0, 1)
            for a in range(4):
                if a == 2:
                    deviations(NORM[1, 0])
                    normalize(NORM[1, 0], 0)
                    for h in range(2):
                        norm(NORM[1, 0], 0, h)
                spread(a)
                numerators(a)
                if a < 3:
                    values(a + 1)
                if a == 0:
                    deviations(NORM["a", 1])
                    normalize(NORM["a", 1], 1)
                    for h in range(2):
                        norm(NORM["a", 1], 1, h)
                if a < 3:
                    first_tap(a + 1)
            experts(1)
            for g in range(GROUPS):
                probability(1, g)

        @block.vector
        def _(v):
            steps = [0]

            def link(ins):
                steps[0] += 1
                ins.then_inc(dve_step, 1)
                v.wait_ge(dve_step, steps[0])

            def stats(k, g):
                for t in range(GT):
                    last = nc.vector.bn_stats(bn[:, t, :], x[:, g * GT + t, :])
                link(last)
                for t in range(GT):
                    last = nc.vector.bn_aggr(mv[:, t, :], bn[:, t, :])
                last.then_inc(stats_ready, 1)

            def normalize(k, g):
                v.wait_ge(std_ready, k + 1)
                if k:
                    v.wait_ge(xn_ready[1], k)
                link(nc.vector.reciprocal(rstd[:], std[:]))
                nc.vector.scalar_tensor_tensor(out=shift[:], in0=mv[:, :, 0], scalar=-1.0, in1=rstd[:],
                                               op0=ALU.mult, op1=ALU.mult).then_inc(scale_ready, 1)
                v.wait_ge(scale_ready, k + 1)
                if k in BEFORE:
                    v.wait_ge(xn_turned, 2 * BEFORE[k] + 2)
                for t in range(GT // 2):
                    last = nc.vector.tensor_scalar(xn[g][:, t, :], x[:, g * GT + t, :], rstd[:, t:t + 1], shift[:, t:t + 1],
                                                   ALU.mult, ALU.add)
                last.then_inc(xn_ready[0], 1)

            def split(k, f, g):
                for h in range(2):
                    v.wait_ge(xn_ready[h], k + 1)
                link(nc.vector.tensor_copy(xs[g][:, :, 0:D], xn[g][:]))
                nc.vector.tensor_tensor(xs[g][:, :, D:2 * D], xn[g][:], xs[g][:, :, 0:D], ALU.subtract).then_inc(xs_ready, 1)

            def choose(f, g):
                n = GROUPS * f + g
                v.wait_ge(logits_ready, n + 1)
                all3 = [P, GT, EXPERTS]
                link(nc.vector.tensor_tensor(lg[:], bank[5][:, 0:GE].rearrange("p (t e) -> p t e", t=GT),
                                             br[:, None, :].to_broadcast(all3), ALU.add))
                link(nc.vector.tensor_reduce(top[:], lg[:], X, ALU.max))
                nc.vector.tensor_tensor(ld[g][:], lg[:], top[:, :, None].to_broadcast(all3), ALU.subtract).then_inc(shifted_ready, 1)
                v.wait_ge(shifted_ready, n + 1)
                link(nc.vector.scalar_tensor_tensor(out=score[:], in0=ld[g][:], scalar=0.0, in1=rank[:, None, :].to_broadcast(all3),
                                                    op0=ALU.is_ge, op1=ALU.mult))
                link(nc.vector.tensor_reduce(best[:], score[:], X, ALU.max))
                nc.vector.tensor_tensor(onehot[:], score[:], best[:, :, None].to_broadcast(all3), ALU.is_equal).then_inc(onehot_ready, 1)

            def weigh(f, g):
                v.wait_ge(exp_ready, GROUPS * f + g + 1)
                link(nc.vector.tensor_reduce(exsum[:], ex[g][:], X, ALU.add))
                link(nc.vector.reciprocal(exsum[:], exsum[:]))
                link(nc.vector.tensor_scalar(coef[g][:], exsum[:], 0.5, None, ALU.mult))

            def place(f, g):
                n = GROUPS * f + g
                all3 = [P, GT, EXPERTS]
                v.wait_ge(ranks_ready, n + 1)
                link(nc.vector.tensor_scalar(cnt[:], bank[5][:, 2 * GE:2 * GE + EXPERTS], float(P - 1), None, ALU.add))
                link(nc.vector.tensor_scalar(tiles[:], cnt[:], P.bit_length() - 1, None, ALU.logical_shift_right))
                link(nc.vector.tensor_tensor_scan(cum[:], ones1[:], tiles[:], 0.0, ALU.mult, ALU.add))
                link(nc.vector.tensor_tensor(first[:], cum[:], tiles[:], ALU.subtract))
                link(nc.vector.tensor_scalar(first[:], first[:], float(P), float(g * GTILES * P), ALU.mult, ALU.add))
                link(nc.vector.tensor_tensor(posw[:], bank[5][:, GE:2 * GE].rearrange("p (t e) -> p t e", t=GT),
                                             first[:, None, :].to_broadcast(all3), ALU.add))
                link(nc.vector.tensor_tensor(posw[:], posw[:], onehot[:], ALU.mult))
                link(nc.vector.tensor_reduce(posf[:], posw[:], X, ALU.add))
                nc.vector.tensor_copy(pos[g][:], posf[:]).then_inc(pos_ready, 1)
                own, tile3 = slice(g * GTILES, (g + 1) * GTILES), [P, GTILES, EXPERTS]
                link(nc.vector.tensor_tensor(over[:], cum[:, None, :].to_broadcast(tile3),
                                             cf[:, C_TILE:C_TILE + GTILES, None].to_broadcast(tile3), ALU.is_le))
                link(nc.vector.tensor_reduce(owner[:], over[:], X, ALU.add))
                nc.vector.tensor_scalar(expert[:, own], owner[:], float(EXPERTS - 1), None, ALU.min).then_inc(expert_ready, 1)
                nc.vector.tensor_scalar(isrow[:, own], owner[:], float(EXPERTS - 1), cf[:, C_PART + 2:C_PART + 3],
                                        ALU.min, ALU.is_equal).then_inc(isrow_ready, 1)

            def bias_rest(part, out):
                v.wait_ge(bias_step, 2 * part + 2)
                of = bf if part == 0 else bres
                return nc.vector.scalar_tensor_tensor(out=out[:], in0=bhi[:], scalar=cf[:, C_PART + part:C_PART + part + 1],
                                                      in1=of[:], op0=ALU.mult, op1=ALU.add)

            def low_halves(weights, high, high_done, h, own):
                v.wait_ge(high_done, h + 1)
                nc.vector.scalar_tensor_tensor(out=table[:, own, high + HIDDEN:high + 2 * HIDDEN], in0=weights[:, own, :],
                                               scalar=WSCALE, in1=table[:, own, high:high + HIDDEN],
                                               op0=ALU.mult, op1=ALU.subtract).then_inc(low_dve, 1)

            def act_split(f, i, s):
                n, r = f * NT + i * TURN + s, s % RING
                v.wait_ge(gelu_ready, n + 1)
                if later(f, i) or s >= RING:
                    v.wait_ge(y_ready, n + (1 - RING))
                nc.vector.tensor_copy(acth[:, r, :], act[:, r, :]).then_inc(acth_ready, 1)
                v.wait_ge(acth_ready, n + 1)
                nc.vector.tensor_tensor(actl[:, r, :], act[:, r, :], acth[:, r, :], ALU.subtract).then_inc(actl_ready, 1)

            def copy_weights(f, i, s):
                e = v.value_load(expert[0:1, bass.ds(i * TURN + s, 1)], min_val=0, max_val=EXPERTS - 1)
                if later(f, i):
                    v.wait_ge(y_ready, f * NT + i * TURN + (s + 1 - TURN))
                nc.vector.tensor_copy(ringW[:, s, :], table[:, bass.ds(e, 1), :])
                nc.vector.tensor_copy(ring32[:, s, WCOLS // 2:], rows32[:, bass.ds(e, 1), WCOLS // 2:]).then_inc(w_copied, 1)

            def copies(f, i, s, last=False):
                if s + RING in COPIED:
                    copy_weights(f, i, s + RING)
                elif s + RING - TURN in COPIED and not last:
                    copy_weights(f, i + 1, s + RING - TURN)

            def experts(f):
                v.wait_ge(expert_ready, GROUPS * f + 1)
                if f == 0:
                    v.wait_ge(low_pool, 1)
                copy_weights(f, 0, COPIED[0])
                for s in range(TURN):
                    copies(f, 0, s)
                    act_split(f, 0, s)
                    if s == 1 and f == 1:
                        split(NORM[f, 1], f, 1)
                    if s == 3 and f == 1:
                        choose(f, 1)
                    if s == 4 and f == 1:
                        place(f, 1)
                    if s == TURN - 1 and f == 0:
                        weigh(0, 0)
                v.wait_ge(expert_ready, GROUPS * f + 2)
                with v.Fori(1, TURNS - 1) as i:
                    for s in range(TURN):
                        copies(f, i, s)
                        act_split(f, i, s)
                for s in range(TURN):
                    copies(f, TURNS - 1, s, last=True)
                    act_split(f, TURNS - 1, s)
                    if f == 0 and s == 0:
                        for h in range(2):
                            add_ffn(0, 0, h)
                    if f == 0 and s == 1:
                        stats(NORM["a", 0], 0)
                    if f == 0 and s == 2:
                        normalize(NORM["a", 0], 0)

            def add_ffn(f, g, h):
                for t in range(4 * h, 4 * h + 4):
                    v.wait_ge(back_done[g][t], 16 * (f + 1))
                    last = nc.vector.scalar_tensor_tensor(out=x[:, g * GT + t, :], in0=yback[g][:, t, :], scalar=coef[g][:, t:t + 1],
                                                          in1=x[:, g * GT + t, :], op0=ALU.mult, op1=ALU.add)
                    if f == 1:
                        last.then_inc(x_final, 1)
                if f == 0:
                    link(last)

            seq3 = [P, 2, SEQ]

            def two(ap):
                return ap.rearrange("p (b s) -> p b s", b=2)

            def times_table(product, b, c):
                return nc.vector.tensor_tensor(two(product[:]), two(bank[b][:]), cf[:, None, c:c + SEQ].to_broadcast(seq3), ALU.mult)

            def rope_q(a):
                v.wait_ge(q_ready, a + 1)
                if a:
                    v.wait_ge(qr_ready, a)
                times_table(t1, 0, C_COST)
                times_table(t2, 1, C_SINT).then_inc(q_used, 1)
                if a < 2:
                    v.wait_ge(q_used, a + 1)
                    nc.vector.tensor_tensor(qr[:, a % 2, :], t1[:], t2[:], ALU.add).then_inc(qr_ready, 1)

            def rope_k(a):
                v.wait_ge(k_ready, a + 1)
                if a:
                    v.wait_ge(kr_ready, a)
                times_table(t3, 2, C_COSR)

                def halves(ap, half):
                    return ap.rearrange("p (b h x j) -> p b h x j", b=2, x=2, j=DK // 2)[:, :, :, half, :]

                sine = cf[:, C_SINR:C_SINR + SEQ].rearrange("p (h x j) -> p h x j", x=2, j=DK // 2)
                for half in range(2):
                    last = nc.vector.tensor_tensor(halves(t4[:], half), halves(bank[2][:], 1 - half),
                                                   sine[:, None, :, half, :].to_broadcast([P, 2, SEQ // DK, DK // 2]), ALU.mult)
                last.then_inc(k_used, 1)
                if a < 2:
                    v.wait_ge(k_used, a + 1)
                    nc.vector.tensor_tensor(kr[:], t3[:], t4[:], ALU.add).then_inc(kr_ready, 1)

            def conv(a):
                v.wait_ge(vpad_ready, a + 1)
                v.wait_ge(tap_ready, a + 1)
                for k in range(1, TAPS):
                    last = nc.vector.scalar_tensor_tensor(out=local[:, a % 2, :, :], in0=vpad[:, a % 2, :, k:k + SEQ], scalar=lepe[:, k:k + 1],
                                                          in1=local[:, a % 2, :, :], op0=ALU.mult, op1=ALU.add)
                    if k < TAPS - 1:
                        link(last)
                last.then_inc(conv_done, 1)

            def mask_kv(a):
                v.wait_ge(kv_ready, a + 1)
                for b in range(2):
                    kv = bank[6][:, b * (P + 1):(b + 1) * (P + 1)]
                    nc.vector.tensor_tensor(kvm[:, b, :], kv[:, 0:P], mask, ALU.mult)
                    last = nc.vector.tensor_scalar(ksm[:, b, :], mask[:, 0:P:DK], kv[:, P:P + 1], None, ALU.mult)
                last.then_inc(kvm_ready, 1)

            def invert(a):
                v.wait_ge(den_ready, a + 1)
                link(nc.vector.tensor_scalar(den[:].rearrange("p t h -> p (t h)"), bank[6][:, 0:4 * HEADS], float(SEQ), None, ALU.add))
                nc.vector.reciprocal(rden[:], den[:]).then_inc(rden_ready, 1)

            def attend(a):
                v.wait_ge(num_copied, a + 1)
                v.wait_ge(rdenT_ready, a + 1)
                nc.vector.tensor_tensor(att[:], num[:], two(bank[6][:]), ALU.mult).then_inc(att_ready, 1)
                v.wait_ge(att_ready, a + 1)
                v.wait_ge(conv_done, a + 1)
                link(nc.vector.tensor_tensor(att[:], att[:], local[:, a % 2, :, :], ALU.add))
                v.wait_ge(gate_copied, a + 1)
                nc.vector.tensor_tensor(att[:], att[:], two(gate[:, a % 2, :]), ALU.mult).then_inc(gated_ready, 1)

            def add_attention(a):
                v.wait_ge(proj_ready, a + 1)
                rows = x[:, 4 * a:4 * a + 4, :]
                nc.vector.tensor_tensor(rows, bank[7][:].rearrange("p (t c) -> p t c", t=4), rows, ALU.add).then_inc(x_updated, 1)

            v.wait_ge(consts_loaded, 16 * 4)
            v.wait_ge(pool_set, 1)
            v.wait_ge(x_in_sem[0], 16)
            stats(0, 0)
            bias_rest(0, bres).then_inc(bias_step, 1)
            normalize(0, 0)
            bias_rest(1, bias).then_inc(bias_ready, 1)
            v.wait_ge(x_in_sem[1], 16)
            stats(1, 1)
            normalize(1, 1)
            split(0, 0, 0)
            choose(0, 0)
            place(0, 0)
            v.wait_ge(b1_loaded, 16)
            nc.vector.tensor_copy(rows32[:, :, WCOLS // 2:], b1[:]).then_inc(low_dve, 1)
            low_halves(w1f, 0, w1_high, 1, HE[1])
            for h in range(4):
                low_halves(w2f, 2 * HIDDEN, w2_high, h, QE[h])
            split(1, 0, 1)
            choose(0, 1)
            place(0, 1)
            experts(0)
            v.wait_ge(attn_loaded, 48)
            rope_q(0)
            rope_k(0)
            mask_kv(0)
            for a in range(4):
                if a == 2:
                    v.wait_ge(x_updated, 2)
                    stats(NORM[1, 0], 0)
                    normalize(NORM[1, 0], 0)
                    split(NORM[1, 0], 1, 0)
                if a < 3 and a != 1:
                    rope_k(a + 1)
                invert(a)
                if a == 1:
                    rope_k(2)
                    conv(1)
                if a < 3:
                    rope_q(a + 1)
                if a == 0:
                    weigh(0, 1)
                    for h in range(2):
                        add_ffn(0, 1, h)
                    stats(NORM["a", 1], 1)
                    normalize(NORM["a", 1], 1)
                if a != 1:
                    conv(a)
                if a == 2:
                    choose(1, 0)
                    place(1, 0)
                attend(a)
                if a < 3:
                    mask_kv(a + 1)
                add_attention(a)
            v.wait_ge(x_updated, 4)
            stats(NORM[1, 1], 1)
            normalize(NORM[1, 1], 1)
            experts(1)
            for g in range(GROUPS):
                weigh(1, g)
                for h in range(2):
                    add_ffn(1, g, h)

        @block.tensor
        def _(pe):
            def norm(k, g, h):
                pe.wait_ge(xn_ready[h], k + 1)
                if k == 2 and h == 1:
                    pe.wait_ge(tileT_ready, NT)
                if k:
                    pe.wait_ge(xnT_ready, 2 * k + h)
                    if h == 0:
                        pe.wait_ge(pos_ready, ROUTED[k])
                for t in range(4):
                    last = nc.tensor.transpose(bank[norm_bank(k, h)][:, t * P:(t + 1) * P], xn[g][:, 4 * h + t, :], ident)
                last.then_inc(xn_turned, 1)

            def logits(k, f, g):
                pe.wait_ge(xnT_ready, 2 * k + 2)
                for t in range(GT):
                    last = nc.tensor.matmul(bank[5][:, t * EXPERTS:(t + 1) * EXPERTS], xnT[g][:, t * P:(t + 1) * P], wr[:],
                                            start=True, stop=True)
                last.then_inc(logits_ready, 1)

            def ranks(f, g):
                pe.wait_ge(onehot_ready, GROUPS * f + g + 1)
                hot = onehot[:].rearrange("p t e -> p (t e)")
                nc.tensor.matmul(bank[5][:, GE:2 * GE], before, hot, start=True, stop=False, skip_group_check=True)
                for d in range(1, GT):
                    nc.tensor.matmul(bank[5][:, GE + d * EXPERTS:2 * GE], ones16, hot[:, 0:GE - d * EXPERTS], start=False, stop=False,
                                     skip_group_check=True)
                for t in range(GT):
                    last = nc.tensor.matmul(bank[5][:, 2 * GE:2 * GE + EXPERTS], ones16, onehot[:, t, :], start=False,
                                            stop=(t == GT - 1), skip_group_check=True)
                last.then_inc(ranks_ready, 1)

            def turn(f, i, s):
                n = f * NT + i * TURN + s
                if s % RING == 0:
                    pe.wait_ge(x_landed[s // RING], f * (16 * TURNS) + i * 16 + 16)
                if later(f, i) or s > 0:
                    pe.wait_ge(tileT_ready, n)
                xt = bank[6 + s % 2][:, 0:P].bitcast(F16)
                for k in range(2):
                    last = nc.tensor.transpose(xt[:, k * P:(k + 1) * P], ringX[:, s, k * D:(k + 1) * D], ident16)
                last.then_inc(tile_turned, 1)

            def hidden(f, i, s):
                n = f * NT + i * TURN + s
                if s in COPIED:
                    k = len(COPIED)
                    pe.wait_ge(w_copied, f * (k * TURNS) + i * k + (COPIED.index(s) + 1))
                else:
                    pe.wait_ge(w_landed[s], f * (16 * TURNS) + i * 16 + 16)
                pe.wait_ge(tileT_ready, n + 1)
                if later(f, i) or s >= RING:
                    pe.wait_ge(gelu_ready, n + (1 - RING))
                hb, w, r = bank[s % RING], ringW[:, s, :], s % RING
                xh, xl = ringT[:, r, 0:P], ringT[:, r, P:2 * P]
                for c in range(HC):
                    o = hb[:, c * P:(c + 1) * P]
                    hi, lo = w[:, c * P:(c + 1) * P], w[:, HIDDEN + c * P:HIDDEN + (c + 1) * P]
                    nc.tensor.matmul(o, hi, xh, start=(c == 0), stop=False, skip_group_check=True)
                    nc.tensor.matmul(o, hi, xl, start=False, stop=False, skip_group_check=True)
                    last = nc.tensor.matmul(o, lo, xh, start=False, stop=(c == HC - 1), skip_group_check=True)
                last.then_inc(hid_ready, 1)

            def project(f, i, s):
                n, r = f * NT + i * TURN + s, s % RING
                pe.wait_ge(actl_ready, n + 1)
                if later(f, i) or s >= 2:
                    pe.wait_ge(y_copied, n - 1)
                o, w = bank[3 + s % 2][:, 0:D], ringW[:, s, 2 * HIDDEN:]
                nc.tensor.matmul(o, isrow[:, bass.ds(i * TURN + s, 1)].to_broadcast([P, P]), bias[:], start=True, stop=False)
                for c in range(HC):
                    hi, lo = w[:, c * P:(c + 1) * P], w[:, HIDDEN + c * P:HIDDEN + (c + 1) * P]
                    ah, al = acth[:, r, c * P:(c + 1) * P], actl[:, r, c * P:(c + 1) * P]
                    nc.tensor.matmul(o, ah, hi, start=False, stop=False)
                    nc.tensor.matmul(o, ah, lo, start=False, stop=False)
                    last = nc.tensor.matmul(o, al, hi, start=False, stop=(c == HC - 1))
                last.then_inc(y_ready, 1)

            def step(f, i, s, first=False, last=False):
                if not last or s + 3 < TURN:
                    turn(f, *ahead(i, s, 3))
                if not last or s + 2 < TURN:
                    hidden(f, *ahead(i, s, 2))
                if first and f == 1 and s < 2:
                    norm(NORM[f, 1], 1, s)
                if first and s == 2 and f == 1:
                    logits(NORM[f, 1], f, 1)
                if first and s == 3 and f == 1:
                    ranks(f, 1)
                if last and f == 0 and s in (3, 4):
                    norm(NORM["a", 0], 0, s - 3)
                if last and f == 0 and s == 5:
                    queries(0)
                project(f, i, s)

            def experts(f):
                for s in range(3):
                    turn(f, 0, s)
                if f == 0:
                    pe.wait_ge(bias_ready, 1)
                pe.wait_ge(isrow_ready, GROUPS * f + 1)
                for s in range(2):
                    hidden(f, 0, s)
                for s in range(TURN):
                    step(f, 0, s, first=True)
                pe.wait_ge(isrow_ready, GROUPS * f + 2)
                with pe.Fori(1, TURNS - 1) as i:
                    for s in range(TURN):
                        step(f, i, s)
                for s in range(TURN):
                    step(f, TURNS - 1, s, last=True)

            def transposed(a, t=None):
                xt = xnT[a // 2][:, (a % 2) * HALF:(a % 2 + 1) * HALF]
                return xt if t is None else xt[:, t * P:(t + 1) * P]

            def rows_of(b, w, a):
                for t in range(4):
                    last = nc.tensor.matmul(bank[b][:, t * P:(t + 1) * P], transposed(a, t), wattn[:, w, :], start=True, stop=True)
                return last

            def queries(a):
                if a:
                    pe.wait_ge(q_used, a)
                    pe.wait_ge(gate_copied, a)
                else:
                    pe.wait_ge(attn_loaded, 48)
                    pe.wait_ge(gelu_ready, NT)
                pe.wait_ge(xnT_ready, 2 * NORM["a", a // 2] + a % 2 + 1)
                nc.tensor.matmul(bank[0][:], wattn[:, 0, :], transposed(a), start=True, stop=True)
                nc.tensor.matmul(bank[1][:], wattn[:, 1, :], transposed(a), start=True, stop=True).then_inc(q_ready, 1)

            def keys(a):
                if a:
                    pe.wait_ge(k_used, a)
                rows_of(2, 4, a).then_inc(k_ready, 1)

            def values_by_rows(a):
                if a:
                    pe.wait_ge(vrow_copied, a)
                rows_of(3, 2, a).then_inc(vrow_ready, 1)

            def values_gate(a):
                if a:
                    pe.wait_ge(vpad_ready, a)
                nc.tensor.matmul(bank[4][:], wattn[:, 2, :], transposed(a), start=True, stop=True).then_inc(v_ready, 1)
                pe.wait_ge(q_used, a + 1)
                nc.tensor.matmul(bank[1][:], wattn[:, 3, :], transposed(a), start=True, stop=True).then_inc(gate_ready, 1)

            def keys_values(a):
                pe.wait_ge(kr_ready, a + 1)
                pe.wait_ge(vrow_copied, a + 1)
                if a:
                    pe.wait_ge(att_ready, a)
                for b in range(2):
                    for t in range(2):
                        last = nc.tensor.matmul(bank[6][:, b * (P + 1):(b + 1) * (P + 1)], kr[:, (2 * b + t) * P:(2 * b + t + 1) * P],
                                                vrow[:, 2 * b + t, :], start=(t == 0), stop=(t == 1))
                last.then_inc(kv_ready, 1)

            def fractions(a):
                pe.wait_ge(qr_ready, a + 1)
                pe.wait_ge(kvm_ready, a + 1)
                for t in range(4):
                    last = nc.tensor.matmul(bank[6][:, t * HEADS:(t + 1) * HEADS], qr[:, a % 2, t * P:(t + 1) * P], ksm[:, t // 2, :],
                                            start=True, stop=True)
                last.then_inc(den_ready, 1)
                if a:
                    pe.wait_ge(x_updated, a)
                for b in range(2):
                    nc.tensor.matmul(bank[7][:, b * SEQ:(b + 1) * SEQ], kvm[:, b, :], qr[:, a % 2, b * SEQ:(b + 1) * SEQ],
                                     start=True, stop=True).then_inc(num_ready, 1)

            def turn_reciprocals(a):
                pe.wait_ge(rspread_ready, a + 1)
                for t in range(4):
                    last = nc.tensor.transpose(bank[6][:, t * P:(t + 1) * P],
                                               rspread[:, t * HEADS:(t + 1) * HEADS, :].rearrange("p h d -> p (h d)"), ident)
                last.then_inc(rdenT_ready, 1)

            def output(a):
                pe.wait_ge(gated_ready, a + 1)
                for t in range(4):
                    last = nc.tensor.matmul(bank[7][:, t * P:(t + 1) * P], att[:, t // 2, (t % 2) * P:(t % 2 + 1) * P], wattn[:, 5, :],
                                            start=True, stop=True)
                last.then_inc(proj_ready, 1)

            pe.wait_ge(consts_loaded, 16 * 4)
            for h in range(2):
                norm(0, 0, h)
            logits(0, 0, 0)
            ranks(0, 0)
            for h in range(2):
                norm(1, 1, h)
            logits(1, 0, 1)
            ranks(0, 1)
            experts(0)
            keys(0)
            pe.wait_ge(y_copied, NT)
            values_by_rows(0)
            values_gate(0)
            keys_values(0)
            for a in range(4):
                if a < 3:
                    keys(a + 1)
                if a == 1:
                    fractions(a)
                if a < 3:
                    queries(a + 1)
                if a == 2:
                    for h in range(2):
                        norm(NORM[1, 0], 0, h)
                if a != 1:
                    fractions(a)
                if a == 2:
                    logits(NORM[1, 0], 1, 0)
                if a < 3:
                    values_by_rows(a + 1)
                turn_reciprocals(a)
                if a == 2:
                    ranks(1, 0)
                if a < 3:
                    values_gate(a + 1)
                if a == 0:
                    for h in range(2):
                        norm(NORM["a", 1], 1, h)
                if a < 3:
                    keys_values(a + 1)
                output(a)
            pe.wait_ge(q_used, 4)
            pe.wait_ge(gate_copied, 4)
            pe.wait_ge(x_updated, 4)
            experts(1)


def kernel(**inputs):
    import concourse.bacc as bacc
    from concourse.bass_utils import run_bass_kernel_spmd

    def arr(name):
        return np.ascontiguousarray(inputs[name])

    def turned(name):
        return np.asarray(inputs[name]).T

    swap = (np.arange(P) // DK) * DK + (np.arange(P) + DK // 2) % DK
    q, k = turned("L0_attn_Wq"), turned("L0_attn_Wk")
    wattn = np.stack([q, q[:, swap], turned("L0_attn_Wv"), turned("L0_attn_Wg"), k, turned("L0_attn_Wo")], axis=1)
    lepe = np.concatenate([arr("L0_attn_lepe_w").reshape(D, TAPS), arr("L0_attn_lepe_b").reshape(D, 1)], axis=1)
    b1 = np.ascontiguousarray(arr("L0_ffn_b1").reshape(EXPERTS, HC, P).transpose(2, 0, 1))
    b2 = np.tile(arr("L0_ffn_b2"), (3, 1))
    cf, ch = constants()
    arrays = {
        "x_in": arr("L0_attn_hidden_states").reshape(TOKENS, D),
        "wr_in": arr("L0_ffn_Wr"), "br_in": arr("L0_ffn_br").reshape(1, EXPERTS),
        "w1_in": arr("L0_ffn_W1"), "b1_in": b1, "w2_in": arr("L0_ffn_W2"), "b2_in": b2,
        "wattn_in": np.ascontiguousarray(wattn), "lepe_in": np.ascontiguousarray(lepe), "cf_in": cf, "ch_in": ch,
    }
    nc = bacc.Bacc("TRN2", target_bir_lowering=False, num_devices=1)
    args = [nc.dram_tensor(n, a.shape, mybir.dt.from_np(a.dtype), kind="ExternalInput").ap() for n, a in arrays.items()]
    out = nc.dram_tensor("out", [TOKENS, D], F32, kind="ExternalOutput").ap()
    program(nc, *args, out)
    r = run_bass_kernel_spmd(nc, [arrays], core_ids=[0])
    return r.results[0]["out"].reshape(TOKENS // SEQ, SEQ, D)
```
